# Optimizing a Trainium2 kernel written in Bass

```python
import numpy as np
import jax
import jax.numpy as jnp

def _softmax(x, axis=-1):
    return jax.nn.softmax(x, axis=axis)

def _gelu(x):
    return jax.nn.gelu(x, approximate=True)

def _silu(x):
    return jax.nn.silu(x)

def _sigmoid(x):
    return jax.nn.sigmoid(x)

def _layernorm(x, axis=-1, eps=1e-05):
    m = jnp.mean(x, axis=axis, keepdims=True)
    v = jnp.var(x, axis=axis, keepdims=True)
    return (x - m) / jnp.sqrt(v + eps)

def _scatter_add(tgt, idx, src, axis=0):
    return tgt.at[idx].add(src)

def _segment_sum(src, seg, n):
    return jax.ops.segment_sum(src, seg, n)
kernel_name = 'mk_xattn_ffn_d1_seqx_r2_273e36'

def setup_inputs(seed: int=0):
    np.random.seed(seed)
    _w = jnp.asarray

    def _rec_inputs():
        import jax
        import jax.numpy as jnp
        _rk = jax.random.key(seed)
        x = -0.0002928 + 1 * jax.random.normal(jax.random.fold_in(_rk, 1), (4, 1024, 512), jnp.float32)
        _lenS = 1024 - jax.random.randint(jax.random.fold_in(_rk, 7), (4,), 0, max(1, 1024 // 4) + 1, jnp.int32)
        _lenS2 = 1024 - jax.random.randint(jax.random.fold_in(_rk, 8), (4,), 0, max(1, 1024 // 4) + 1, jnp.int32)
        _ctx_1024P = jax.random.normal(jax.random.fold_in(_rk, 11), (4, 16, 512), jnp.float32)
        _ctx_1024c = jax.random.dirichlet(jax.random.fold_in(_rk, 511), 0.3 * jnp.ones((16,), jnp.float32), (4, 1024))
        _ctx_1024t = jnp.einsum('bsk,bkd->bsd', _ctx_1024c, _ctx_1024P)
        _ctx_1024t = _ctx_1024t * jax.lax.rsqrt(jnp.mean(jnp.square(_ctx_1024t)) + 1e-12) * 0.953939
        ctx_1024 = -1.39393e-06 + 0.999914 * (_ctx_1024t + 0.3 * jax.random.normal(jax.random.fold_in(_rk, 611), (4, 1024, 512), jnp.float32))
        _validS = jnp.arange(1024)[None, :] < _lenS[:, None]
        _validS2 = jnp.arange(1024)[None, :] < _lenS2[:, None]
        _causal = jnp.tril(jnp.ones((1024, 1024), dtype=bool))
        mask_Bx1xSxS2_bf1 = jnp.ones((4, 1, 1024, 1024), dtype=bool)
        return (x, ctx_1024, mask_Bx1xSxS2_bf1)
    x, ctx_1024, mask_Bx1xSxS2_bf1 = _rec_inputs()

    def _L0_xattn_setup():
        import jax, jax.numpy as jnp
        import numpy as np
        D_MODEL = 512
        H = 16
        D_K = D_MODEL // H
        MAX_SEQ_LEN = 1024
        B = 2
        S = 1024
        key = jax.random.key(seed)
        ks = jax.random.split(key, 8)
        scale = 1.0 / np.sqrt(D_MODEL)
        return {'q': jax.random.normal(ks[0], (B, S, D_MODEL), jnp.float32), 'k': jax.random.normal(ks[1], (B, S, D_MODEL), jnp.float32), 'v': jax.random.normal(ks[2], (B, S, D_MODEL), jnp.float32), 'mask': jnp.ones((B, 1, S, S), dtype=bool), 'w_q': jax.random.normal(ks[3], (D_MODEL, D_MODEL), jnp.float32) * scale, 'w_k': jax.random.normal(ks[4], (D_MODEL, D_MODEL), jnp.float32) * scale, 'w_v': jax.random.normal(ks[5], (D_MODEL, D_MODEL), jnp.float32) * scale, 'w_o': jax.random.normal(ks[6], (D_MODEL, D_MODEL), jnp.float32) * scale, 'rel_emb': jax.random.normal(ks[7], (2 * MAX_SEQ_LEN - 1, H), jnp.float32) * 0.02}
    _L0_xattn_all = _L0_xattn_setup()
    _L0_xattn_in = {k: v for k, v in _L0_xattn_all.items() if k in ('w_q', 'w_k', 'w_v', 'w_o', 'rel_emb')}
    del _L0_xattn_all

    def _L0_ffn_setup():
        import jax, jax.numpy as jnp
        import numpy as np
        NUM_EXPERTS = 8
        D_MODEL = 512
        D_FF = 2048
        BATCH, SEQ = (2, 2048)
        key = jax.random.key(seed)
        k_x, k_w1, k_w2 = jax.random.split(key, 3)
        x = jax.random.normal(k_x, (BATCH, SEQ, D_MODEL), dtype=jnp.float32)
        w1 = jax.random.normal(k_w1, (NUM_EXPERTS, D_MODEL, D_FF), dtype=jnp.float32) * (1.0 / np.sqrt(D_MODEL))
        b1 = jnp.zeros((NUM_EXPERTS, D_FF), dtype=jnp.float32)
        w2 = jax.random.normal(k_w2, (NUM_EXPERTS, D_FF, D_MODEL), dtype=jnp.float32) * (1.0 / np.sqrt(D_FF))
        b2 = jnp.zeros((NUM_EXPERTS, D_MODEL), dtype=jnp.float32)
        return {'x': x, 'w1': w1, 'b1': b1, 'w2': w2, 'b2': b2}
    _L0_ffn_all = _L0_ffn_setup()
    _L0_ffn_in = {k: v for k, v in _L0_ffn_all.items() if k in ('w1', 'b1', 'w2', 'b2')}
    del _L0_ffn_all
    return {'x': x, 'ctx_1024': ctx_1024, 'mask_Bx1xSxS2_bf1': mask_Bx1xSxS2_bf1, 'L0_xattn_w_q': _L0_xattn_in['w_q'], 'L0_xattn_w_k': _L0_xattn_in['w_k'], 'L0_xattn_w_v': _L0_xattn_in['w_v'], 'L0_xattn_w_o': _L0_xattn_in['w_o'], 'L0_xattn_rel_emb': _L0_xattn_in['rel_emb'], 'L0_ffn_w1': _L0_ffn_in['w1'], 'L0_ffn_b1': _L0_ffn_in['b1'], 'L0_ffn_w2': _L0_ffn_in['w2'], 'L0_ffn_b2': _L0_ffn_in['b2']}

def reference(x, ctx_1024, mask_Bx1xSxS2_bf1, L0_xattn_w_q, L0_xattn_w_k, L0_xattn_w_v, L0_xattn_w_o, L0_xattn_rel_emb, L0_ffn_w1, L0_ffn_b1, L0_ffn_w2, L0_ffn_b2):
    import jax
    import jax.numpy as jnp

    def _L0_xattn_ref(q, k, v, mask, w_q, w_k, w_v, w_o, rel_emb):
        import jax, jax.numpy as jnp
        import numpy as np
        D_MODEL = 512
        H = 16
        D_K = D_MODEL // H
        MAX_SEQ_LEN = 1024
        B = 2
        S = 1024
        batch, seq_len, _ = q.shape
        query = (q @ w_q.T).reshape(batch, seq_len, H, D_K).transpose(0, 2, 1, 3)
        key_ = (k @ w_k.T).reshape(batch, seq_len, H, D_K).transpose(0, 2, 1, 3)
        value = (v @ w_v.T).reshape(batch, seq_len, H, D_K).transpose(0, 2, 1, 3)
        scores = jnp.einsum('bhqd,bhkd->bhqk', query, key_) / jnp.sqrt(jnp.float32(D_K))
        rng = jnp.arange(seq_len)
        rel_pos = rng[:, None] - rng[None, :] + (MAX_SEQ_LEN - 1)
        rel_bias = rel_emb[rel_pos]
        scores = scores + rel_bias.transpose(2, 0, 1)[None]
        scores = jnp.where(mask, scores, -1000000000.0)
        attn = jax.nn.softmax(scores, axis=-1)
        x = jnp.einsum('bhqk,bhkd->bhqd', attn, value)
        x = x.transpose(0, 2, 1, 3).reshape(batch, seq_len, H * D_K)
        return x @ w_o.T

    def _L0_ffn_ref(x, w1, b1, w2, b2):
        import jax, jax.numpy as jnp
        import numpy as np
        NUM_EXPERTS = 8
        D_MODEL = 512
        D_FF = 2048
        BATCH, SEQ = (2, 2048)
        B, S, D = x.shape
        E = w1.shape[0]
        T = B * S // E
        tokens = x.reshape(E, T, D)
        h = jnp.einsum('etd,edf->etf', tokens, w1) + b1[:, None, :]
        h = jax.nn.gelu(h)
        y = jnp.einsum('etf,efd->etd', h, w2) + b2[:, None, :]
        return y.reshape(B, S, D)
    x = x + _L0_xattn_ref(_layernorm(x, axis=-1), ctx_1024, ctx_1024, mask_Bx1xSxS2_bf1, L0_xattn_w_q, L0_xattn_w_k, L0_xattn_w_v, L0_xattn_w_o, L0_xattn_rel_emb)
    x = x + _L0_ffn_ref(_layernorm(x, axis=-1), L0_ffn_w1, L0_ffn_b1, L0_ffn_w2, L0_ffn_b2)
    return x

_drawn_inputs = setup_inputs


def setup_inputs(seed=0):
    import zlib

    import numpy as np

    out = dict(_drawn_inputs(seed))
    spreads = {'L0_ffn_b1': (0.0, 0.1), 'L0_ffn_b2': (0.0, 0.1)}
    factors = {'L0_xattn_rel_emb': 64.0}
    for name, (base, spread) in spreads.items():
        noise = np.random.default_rng([zlib.crc32(name.encode()), seed]).standard_normal(out[name].shape)
        drawn = base * np.exp(spread * noise) if base else spread * noise
        out[name] = jnp.asarray(drawn.astype(out[name].dtype))
    for name, factor in factors.items():
        out[name] = (out[name] * factor).astype(out[name].dtype)
    return out
```

```python
from contextlib import ExitStack

import concourse.bass as bass
from concourse import mybir

ALU = mybir.AluOpType
ACT = mybir.ActivationFunctionType
AXIS = mybir.AxisListType
F32 = mybir.dt.float32
F16 = mybir.dt.float16
BF16 = mybir.dt.bfloat16
I32 = mybir.dt.int32
U8 = mybir.dt.uint8

P = 128
DMA = 16
HI, LO = 0, 1
EPS = 1e-5

WEIGHT_SCALE = 64.0
OUT_SCALE = 16.0
SCORE_SCALE = 4.0
MASKED = -(2.0**100)


class Shapes:
    def __init__(self, x, rel_emb, w1):
        self.B, self.S, self.D = x.shape
        self.H = rel_emb.shape[1]
        self.DK = self.D // self.H
        self.E, _, self.F = w1.shape
        self.T = self.B * self.S
        self.KT = self.D // P
        self.CH = 512
        self.NCH = self.T // self.CH
        self.TT = self.CH // P
        self.HG = P // self.DK
        self.NH = self.B * self.H
        self.QT = self.S // P
        self.REL = 2 * self.S
        self.SKEW = self.S + self.S - P
        self.FT = self.F // P
        assert self.DK == 32 and self.CH == self.T // self.E and self.D == 512 and self.S % self.CH == 0


PASSES = [(HI, HI), (HI, LO), (LO, HI)]


def later(c):
    return not isinstance(c, int) or c > 0


def settle(eng, gate):
    eng.sem_inc(gate, 1)


def project_phase(nc, s, io, scratch, keep):
    KT, TT, CH, D, NCH, QT = s.KT, s.TT, s.CH, s.D, s.NCH, s.QT
    with ExitStack() as ctx:
        sb = lambda name, shape, dt: ctx.enter_context(nc.sbuf_tensor(name, shape, dt))
        sem = lambda name: ctx.enter_context(nc.semaphore(name))
        w_raw = sb("w_raw", [P, 4, KT, D], F32)
        wT = sb("wT", [P, 3, 2, KT, D], F16)
        rel_raw = sb("rel_raw", [P, s.REL // P, s.H], F32)
        rel_rev = sb("rel_rev", [s.H, s.REL], F32)
        b1_raw = sb("b1_raw", [s.E * s.FT, P], F32)
        x_in = sb("x_in", [P, TT, D], F32)
        c_in = sb("c_in", [P, TT, D], F32)
        m_in = sb("m_in", [P, TT, s.S], U8)
        stats = sb("stats", [P, TT, 6], F32)
        moments = sb("moments", [P, TT, 2], F32)
        var_eps = sb("var_eps", [P, TT], F32)
        rstd = sb("rstd", [P, TT], F32)
        minus_half = sb("minus_half", [P, TT], F32)
        x_norm = sb("x_norm", [P, TT, D], F32)
        xT = sb("xT", [P, 2, KT, CH], F16)
        cT = sb("cT", [P, 2, KT, CH], F16)
        qk_cut = sb("qk_cut", [P, 4, 2, CH], F16)
        v_out = sb("v_out", [P, 4, D], F32)
        m_new = sb("m_new", [P, 1], F32)
        m_min = sb("m_min", [P, 1], F32)
        ps = ctx.enter_context(nc.psum_tensor("ps_project", [P, 8, 512], F32))

        w_loaded, small_loaded = sem("w_loaded"), sem("small_loaded")
        x_loaded, c_loaded, m_loaded = sem("x_loaded"), sem("c_loaded"), sem("m_loaded")
        consts_ready = sem("consts_ready")
        turned = sem("turned")
        turned_hi, turned_lo = sem("turned_hi"), sem("turned_lo")
        multiplied = sem("multiplied")
        product_hi, product_lo = sem("product_hi"), sem("product_lo")
        pool_gate, dve_gate = sem("pool_gate"), sem("dve_gate")
        stats_done, moments_done = sem("stats_done"), sem("moments_done")
        var_done, rstd_done = sem("var_done"), sem("rstd_done")
        x_normed, mask_read, mask_min_done = sem("x_normed"), sem("mask_read"), sem("mask_min_done")
        b1_turned, b1_kept = sem("b1_turned"), sem("b1_kept")
        rel_rev_stored, q_stored, k_stored, v_stored = (
            sem("rel_rev_stored"), sem("q_stored"), sem("k_stored"), sem("v_stored"))
        flag_turned, flag_kept, rel_zeroed = sem("flag_turned"), sem("flag_kept"), sem("rel_zeroed")

        T_BANKS = M_BANKS = 4
        W_ITEMS = 4 * KT
        REL_ITEMS = s.REL // 512
        SETUP = W_ITEMS + REL_ITEMS
        assert SETUP % T_BANKS == 0
        T_CHUNK = 2 * KT
        M_CHUNK = 3 * TT
        weight_src = [io["wq"], io["wk"], io["wv"], io["wo"]]
        chunk_rows = "(c t p) d -> c p t d"
        x_rows = io["x"].rearrange("b s d -> (b s) d").rearrange(chunk_rows, t=TT, p=P)
        ctx_rows = io["ctx"].rearrange("b s d -> (b s) d").rearrange(chunk_rows, t=TT, p=P)
        mask_rows = io["mask"].rearrange("b o q k -> (b o q) k").rearrange(chunk_rows, t=TT, p=P)

        def wT_of(w, part):
            return keep["woT"][:, part] if w == 3 else wT[:, w, part]

        block = ctx.enter_context(nc.Block())

        @block.gpsimd
        def _(pool):
            ident, exchange, select = keep["ident"], keep["exchange"], keep["select"]
            pool.memset(ident[:], 0.0).then_inc(consts_ready, 1)
            pool.memset(exchange[:], 0.0).then_inc(consts_ready, 1)
            pool.memset(select[:], 1.0).then_inc(consts_ready, 1)
            pool.memset(minus_half[:], -0.5).then_inc(consts_ready, 1)
            pool.wait_ge(consts_ready, 4)
            pool.affine_select(out=ident[:], in_=ident[:], compare_op=ALU.not_equal, fill=1.0, base=0,
                               pattern=[[-1, P]], channel_multiplier=1).then_inc(consts_ready, 1)
            pool.affine_select(out=exchange[:], in_=exchange[:], compare_op=ALU.not_equal, fill=1.0,
                               base=-(P - 1), pattern=[[1, P]], channel_multiplier=1).then_inc(consts_ready, 1)
            pool.affine_select(out=select[:], in_=select[:], compare_op=ALU.is_equal, fill=0.0, base=0,
                               pattern=[[-1, 2], [-2, 4], [0, s.DK]], channel_multiplier=1).then_inc(consts_ready, 1)
            pool.wait_ge(consts_ready, 7)
            pool.tensor_copy(keep["exchange_b"][:], exchange[:]).then_inc(consts_ready, 1)

            def chunk(c):
                if later(c):
                    pool.wait_ge(x_normed, c * TT)
                pool.dma_start(x_in[:], x_rows[c]).then_inc(x_loaded, DMA)
                if later(c):
                    pool.wait_ge(mask_read, c)
                pool.dma_start(m_in[:], mask_rows[c]).then_inc(m_loaded, DMA)
                pool.wait_ge(moments_done, c + 1)
                settle(pool, pool_gate)
                pool.tensor_scalar(var_eps[:], moments[:, :, 1], 1.0, EPS, ALU.mult, ALU.add).then_inc(var_done, 1)
                pool.wait_ge(var_done, c + 1)
                pool.tensor_tensor(rstd[:], var_eps[:], minus_half[:], ALU.pow).then_inc(rstd_done, 1)

            chunk(0)
            with pool.Fori(1, NCH) as c:
                chunk(c)

        @block.scalar
        def _(act):
            for n in range(W_ITEMS):
                w, kt = n // KT, n % KT
                act.wait_ge(turned, n + 1)
                act.activation(wT_of(w, HI)[:, kt], ps[:, n % T_BANKS], ACT.Copy,
                               scale=WEIGHT_SCALE).then_inc(turned_hi, 1)
            for n in range(W_ITEMS, SETUP):
                act.wait_ge(turned, n + 1)
                act.activation(rel_rev[:, (n - W_ITEMS) * 512:(n - W_ITEMS + 1) * 512], ps[0:s.H, n % T_BANKS],
                               ACT.Copy, scale=SCORE_SCALE).then_inc(turned_hi, 1)
            act.wait_ge(b1_turned, 1)
            act.copy(keep["b1T"][:], ps[:, 4, 0:P]).then_inc(b1_kept, 1)

            def turned_high(c, dst, first):
                for kt in range(KT):
                    act.wait_ge(turned, SETUP + c * T_CHUNK + first + kt + 1)
                    act.copy(dst[:, HI, kt], ps[:, kt % T_BANKS]).then_inc(turned_hi, 1)

            def project_high(c, which):
                for j in range(TT):
                    item = which * TT + j
                    act.wait_ge(multiplied, c * M_CHUNK + item + 1)
                    bank = ps[:, 4 + item % M_BANKS]
                    if which == 1:
                        if later(c):
                            act.wait_ge(v_stored, c * TT * DMA)
                        act.activation(v_out[:, j], bank, ACT.Copy, scale=1 / WEIGHT_SCALE).then_inc(product_hi, 1)
                    else:
                        if which == 2:
                            act.wait_ge(k_stored, (c + 1) * TT * DMA)
                        elif later(c):
                            act.wait_ge(q_stored, c * TT * DMA)
                        scale = 1 / WEIGHT_SCALE if which == 0 else SCORE_SCALE * s.DK**-0.5 / WEIGHT_SCALE
                        act.activation(qk_cut[:, j, HI], bank, ACT.Copy, scale=scale).then_inc(product_hi, 1)

            turned_high(0, cT, 0)
            turned_high(0, xT, KT)

            def chunk(c, more):
                project_high(c, 0)
                project_high(c, 1)
                if more:
                    turned_high(c + 1, cT, 0)
                project_high(c, 2)
                if more:
                    turned_high(c + 1, xT, KT)

            chunk(0, True)
            with act.Fori(1, NCH - 1) as c:
                chunk(c, True)
            chunk(NCH - 1, False)

        @block.vector
        def _(dve):
            dve.memset(rel_raw[:], 0.0).then_inc(rel_zeroed, 1)
            for n in range(W_ITEMS):
                w, kt = n // KT, n % KT
                dve.wait_ge(turned_hi, n + 1)
                dve.scalar_tensor_tensor(out=wT_of(w, LO)[:, kt], in0=ps[:, n % T_BANKS], scalar=WEIGHT_SCALE,
                                         in1=wT_of(w, HI)[:, kt], op0=ALU.mult, op1=ALU.subtract).then_inc(turned_lo, 1)

            def normalize(c):
                dve.wait_ge(x_loaded, (c + 1) * DMA)
                for t in range(TT):
                    dve.bn_stats(stats[:, t], x_in[:, t]).then_inc(stats_done, 1)
                dve.wait_ge(stats_done, (c + 1) * TT)
                settle(dve, dve_gate)
                for t in range(TT):
                    ins = dve.bn_aggr(moments[:, t], stats[:, t])
                ins.then_inc(moments_done, 1)
                dve.wait_ge(m_loaded, (c + 1) * DMA)
                dve.tensor_reduce(m_new[:], m_in[:], AXIS.XY, ALU.min).then_inc(mask_read, 1)
                dve.wait_ge(mask_read, c + 1)
                dve.tensor_tensor(m_min[:], m_min[:], m_new[:], ALU.min).then_inc(mask_min_done, 1)
                dve.wait_ge(mask_min_done, c + 2)
                dve.wait_ge(rstd_done, c + 1)
                if not isinstance(c, int):
                    dve.wait_ge(turned, SETUP + c * T_CHUNK)
                for t in range(TT):
                    dve.tensor_scalar(x_norm[:, t], x_in[:, t], moments[:, t, 0:1], rstd[:, t:t + 1],
                                      ALU.subtract, ALU.mult).then_inc(x_normed, 1)

            def turned_low(c, dst, first):
                for kt in range(KT):
                    dve.wait_ge(turned_hi, SETUP + c * T_CHUNK + first + kt + 1)
                    dve.tensor_tensor(dst[:, LO, kt], ps[:, kt % T_BANKS], dst[:, HI, kt],
                                      ALU.subtract).then_inc(turned_lo, 1)

            def project_low(c, which):
                for j in range(TT):
                    item = which * TT + j
                    dve.wait_ge(product_hi, c * M_CHUNK + item + 1)
                    scale = 1 / WEIGHT_SCALE if which == 0 else SCORE_SCALE * s.DK**-0.5 / WEIGHT_SCALE
                    dve.scalar_tensor_tensor(out=qk_cut[:, j, LO], in0=ps[:, 4 + item % M_BANKS], scalar=scale,
                                             in1=qk_cut[:, j, HI], op0=ALU.mult, op1=ALU.subtract).then_inc(product_lo, 1)

            dve.memset(m_min[:], 1.0).then_inc(mask_min_done, 1)
            dve.wait_ge(mask_min_done, 1)
            normalize(0)
            turned_low(0, cT, 0)
            turned_low(0, xT, KT)

            def chunk(c, more):
                if more:
                    normalize(c + 1)
                project_low(c, 0)
                if more:
                    turned_low(c + 1, cT, 0)
                project_low(c, 2)
                if more:
                    turned_low(c + 1, xT, KT)

            chunk(0, True)
            with dve.Fori(1, NCH - 1) as c:
                chunk(c, True)
            chunk(NCH - 1, False)
            dve.wait_ge(flag_turned, 1)
            dve.tensor_reduce(keep["all_kept"][:], ps[0:1, 0, 0:P], AXIS.X, ALU.min).then_inc(flag_kept, 1)
            dve.wait_ge(flag_kept, 1)

        @block.tensor
        def _(pe):
            ident, exchange = keep["ident"], keep["exchange"]
            pe.wait_ge(consts_ready, 8)
            pe.wait_ge(small_loaded, 3 * DMA)
            pe.transpose(ps[:, 4, 0:P], b1_raw[:], ident[:]).then_inc(b1_turned, 1)
            pe.wait_ge(w_loaded, 4 * DMA)
            for n in range(SETUP):
                w, kt = n // KT, n % KT
                if n >= T_BANKS:
                    pe.wait_ge(turned_hi, n - T_BANKS + 1)
                    if n - T_BANKS < W_ITEMS:
                        pe.wait_ge(turned_lo, n - T_BANKS + 1)
                for j in range(4):
                    if n < W_ITEMS:
                        ins = pe.transpose(ps[:, n % T_BANKS, j * P:(j + 1) * P], w_raw[:, w, j, kt * P:(kt + 1) * P],
                                           ident[:])
                    else:
                        z = (n - W_ITEMS) * 4 + j
                        ins = pe.transpose(ps[0:s.H, n % T_BANKS, j * P:(j + 1) * P],
                                           rel_raw[:, s.REL // P - 1 - z, :], exchange[:])
                ins.then_inc(turned, 1)

            def turn(c, src, perm, first):
                for kt in range(KT):
                    item = c * T_CHUNK + first + kt
                    pe.wait_ge(turned_hi, SETUP + item - T_BANKS + 1)
                    pe.wait_ge(turned_lo, W_ITEMS + item - T_BANKS + 1 if not (isinstance(c, int) and c == 0 and first == 0)
                               else W_ITEMS)
                    for t in range(TT):
                        ins = pe.transpose(ps[:, kt % T_BANKS, t * P:(t + 1) * P], src[:, t, kt * P:(kt + 1) * P], perm[:])
                    ins.then_inc(turned, 1)

            def turn_ctx(c):
                pe.wait_ge(c_loaded, (c + 1) * DMA)
                turn(c, c_in, ident, 0)

            def turn_x(c):
                pe.wait_ge(x_normed, (c + 1) * TT)
                turn(c, x_norm, exchange, KT)

            def bank_free(c, which, j):
                item = which * TT + j
                if which == 0:
                    if later(c):
                        pe.wait_ge(product_hi, c * M_CHUNK)
                        pe.wait_ge(product_lo, c * 2 * TT)
                    return
                pe.wait_ge(product_hi, c * M_CHUNK + item - M_BANKS + 1)
                if which == 1:
                    pe.wait_ge(product_lo, c * 2 * TT + j + 1)

            def project_T(c, which, w, src):
                for j in range(TT):
                    bank_free(c, which, j)
                    bank = ps[:, 4 + (which * TT + j) % M_BANKS]
                    steps = [(kt, a, b) for kt in range(KT) for a, b in PASSES]
                    for n, (kt, a, b) in enumerate(steps):
                        ins = pe.matmul(bank, wT[:, w, a, kt, j * P:(j + 1) * P], src[:, b, kt],
                                        start=(n == 0), stop=(n == len(steps) - 1))
                    ins.then_inc(multiplied, 1)

            def project_v(c):
                for j in range(TT):
                    bank_free(c, 1, j)
                    bank = ps[:, 4 + (TT + j) % M_BANKS]
                    steps = [(kt, a, b) for kt in range(KT) for a, b in PASSES]
                    for n, (kt, a, b) in enumerate(steps):
                        ins = pe.matmul(bank, cT[:, a, kt, j * P:(j + 1) * P], wT[:, 2, b, kt],
                                        start=(n == 0), stop=(n == len(steps) - 1))
                    ins.then_inc(multiplied, 1)

            def chunk(c, more):
                pe.wait_ge(turned_hi, SETUP + c * T_CHUNK + KT)
                pe.wait_ge(turned_lo, W_ITEMS + c * T_CHUNK + KT)
                project_T(c, 0, 1, cT)
                project_v(c)
                if more:
                    turn_ctx(c + 1)
                pe.wait_ge(turned_hi, SETUP + c * T_CHUNK + 2 * KT)
                pe.wait_ge(turned_lo, W_ITEMS + c * T_CHUNK + 2 * KT)
                project_T(c, 2, 0, xT)
                if more:
                    turn_x(c + 1)

            turn_ctx(0)
            turn_x(0)
            pe.wait_ge(b1_kept, 1)
            chunk(0, True)
            with pe.Fori(1, NCH - 1) as c:
                chunk(c, True)
            chunk(NCH - 1, False)
            pe.wait_ge(mask_min_done, NCH + 1)
            pe.wait_ge(turned_hi, SETUP + NCH * T_CHUNK)
            pe.wait_ge(turned_lo, W_ITEMS + NCH * T_CHUNK)
            pe.transpose(ps[0:1, 0, 0:P], m_min[:], ident[:]).then_inc(flag_turned, 1)

        HEAD = s.DK * s.S
        half = s.S // CH

        def store_cut(sp, c, j, scratch_tensor):
            return sp.dma_start(
                bass.AP(scratch_tensor, (c // half) * (s.H * HEAD) + (c % half) * CH + j * s.HG * HEAD,
                        [[s.S, P], [s.NH * HEAD, 2], [1, CH]]), qk_cut[:, j])

        @block.sync
        def _(sp):
            for w in (1, 2, 0, 3):
                sp.dma_start(w_raw[:, w], weight_src[w].rearrange("(o p) i -> p o i", p=P)).then_inc(w_loaded, DMA)
            sp.dma_start(b1_raw[:], io["b1"].rearrange("e (f p) -> (e f) p", p=P)).then_inc(small_loaded, DMA)
            sp.wait_ge(rel_zeroed, 1)
            full = (s.REL // P - 1) * P
            sp.dma_start(rel_raw[:, 0:s.REL // P - 1, :],
                         io["rel_emb"][0:full, :].rearrange("(t p) h -> p t h", p=P)).then_inc(small_loaded, DMA)
            sp.dma_start(rel_raw[0:P - 1, s.REL // P - 1, :], io["rel_emb"][full:, :]).then_inc(small_loaded, DMA)
            sp.dma_start(c_in[:], ctx_rows[0]).then_inc(c_loaded, DMA)
            sp.wait_ge(turned_hi, SETUP)
            for b in range(s.B):
                sp.dma_start(scratch["rel"][b * s.H:(b + 1) * s.H, :], rel_rev[:]).then_inc(rel_rev_stored, DMA)

            def chunk(c, more):
                if more:
                    sp.wait_ge(turned, SETUP + c * T_CHUNK + KT)
                    sp.dma_start(c_in[:], ctx_rows[c + 1]).then_inc(c_loaded, DMA)
                for j in range(TT):
                    sp.wait_ge(product_lo, c * 2 * TT + j + 1)
                    store_cut(sp, c, j, scratch["k"]).then_inc(k_stored, DMA)
                for j in range(TT):
                    sp.wait_ge(product_hi, c * M_CHUNK + TT + j + 1)
                    sp.dma_start(
                        bass.AP(scratch["v"], (c // half) * (s.H * s.S * s.DK) + ((c % half) * CH + j * P) * s.DK,
                                [[s.DK, P], [s.S * s.DK, s.H], [1, s.DK]]), v_out[:, j]).then_inc(v_stored, DMA)
                for j in range(TT):
                    sp.wait_ge(product_lo, c * 2 * TT + TT + j + 1)
                    store_cut(sp, c, j, scratch["q"]).then_inc(q_stored, DMA)

            chunk(0, True)
            with sp.Fori(1, NCH - 1) as c:
                chunk(c, True)
            chunk(NCH - 1, False)
            sp.wait_ge(rel_rev_stored, s.B * DMA)
            for stored in (q_stored, k_stored, v_stored):
                sp.wait_ge(stored, NCH * TT * DMA)


def attend_phase(nc, s, io, scratch, keep):
    NH, S, QT, DK = s.NH, s.S, s.QT, s.DK
    LAG = 3
    HEAD = DK * S
    CHUNKS = 4
    QC = S // CHUNKS

    items, first_item = [], []
    for t in range(QT):
        first_item.append(len(items))
        items += [("half", t, 0), ("half", t, 1)]
        if t == 3:
            items.append(("sums", t, 0))
        if t == 5:
            items.append(("spread", t, 0))
    PER = len(items)
    T_BANKS = 3
    assert PER % T_BANKS == 0
    ACT_HALVES = {(t, 0) for t in range(QT)} | {(4, 1)}

    spread_idx = items.index(("spread", 5, 0))
    sums_idx = items.index(("sums", 3, 0))

    def item_exists_at(n, idx):
        return not isinstance(n, int) or item_exists(n, idx)

    def by_act(idx):
        kind, t, h = items[idx]
        return kind != "half" or (t, h) in ACT_HALVES

    def item_exists(n, idx):
        kind, t, _ = items[idx]
        behind = 1 if kind != "half" or t < LAG else 0
        return 0 <= n - behind < NH

    def count(n, idx, engine=None):
        def upto(m, k):
            return sum(1 for a in range(m + 1) for j in range(PER if a < m else k + 1)
                       if item_exists(a, j) and (engine is None or by_act(j) == (engine == "act")))
        if isinstance(n, int):
            while idx < 0:
                n, idx = n - 1, idx + PER
            return upto(n, idx)
        back = 0
        while idx < 0:
            back, idx = back + 1, idx + PER
        per = upto(4, idx) - upto(3, idx)
        return n * per + (upto(4 - back, idx) - 4 * per)

    def before_in_bank(n, idx):
        back = 0
        k = idx - T_BANKS
        while True:
            m, j = back, k
            while j < 0:
                m, j = m + 1, j + PER
            if not isinstance(n, int):
                return k
            if n - m < 0:
                return None
            if item_exists(n - m, j):
                return k
            k -= T_BANKS

    VALUES_NEXT = {t: t - LAG for t in range(LAG, QT)}
    VALUES_AFTER = {t: QT - LAG + t for t in range(LAG)}

    with ExitStack() as ctx:
        sb = lambda name, shape, dt: ctx.enter_context(nc.sbuf_tensor(name, shape, dt))
        sem = lambda name: ctx.enter_context(nc.semaphore(name))
        q_parts = sb("q_parts", [P, 2, S], F16)
        k_parts = sb("k_parts", [P, 2, S], F16)
        v_head = sb("v_head", [P, 2, QT, DK], F32)
        skew = sb("skew", [P, 2, s.SKEW], F32)
        biased = sb("biased", [P, 4, S], F32)
        neg_max = sb("neg_max", [P, 2 * QT], F32)
        probs = sb("probs", [P, 4, S], F32)
        row_sum = sb("row_sum", [P, 2, QT], F32)
        recip = sb("recip", [P, 2, QT], F32)
        recip_T = sb("recip_T", [QT, P], F32)
        spread = sb("spread", [P, 2, QC], F32)
        probs_T = sb("probs_T", [P, 2, QT, S], F32)
        o_head = sb("o_head", [P, 2, QC], F32)
        o_cut = sb("o_cut", [P, 2, 2, QC], F16)
        mask_u = sb("mask_u", [P, 2, S], U8)
        penalty = sb("penalty", [P, 2, S], BF16)
        ps = ctx.enter_context(nc.psum_tensor("ps_attend", [P, 8, 512], F32))
        values = ps[:, 7, 0:QC]

        pair = lambda name: [sem(f"{name}0"), sem(f"{name}1")]
        q_loaded, k_loaded, v_loaded, skew_loaded = pair("q_in"), pair("k_in"), pair("v_in"), pair("skew_in")
        scores_ready = sem("scores_ready")
        bias_done = sem("bias_done")
        probs_ready = sem("probs_ready")
        item_ready = sem("item_ready")
        read_act, read_dve = sem("read_act"), sem("read_dve")
        recip_done = sem("recip_done")
        values_ready = sem("values_ready")
        o_ready = sem("o_ready")
        o_low = sem("o_low")
        o_high = sem("o_high")
        o_stored = pair("o_out")
        mask_in = pair("mask_in")
        penalty_ready = sem("penalty_ready")
        pool_gate, dve_gate = sem("pool_gate2"), sem("dve_gate2")

        def loops(eng, head, tail):
            for p in range(2):
                head(0, p)
            with eng.Fori(1, NH // 2) as i:
                for p in range(2):
                    head(i, p)
            if tail:
                for p in range(2):
                    head(NH // 2, p)

        def real(n, behind=0):
            return not isinstance(n, int) or 0 <= n - behind < NH

        def wait_read(pe, n, idx):
            prev = before_in_bank(n, idx)
            if prev is None:
                return
            engine = "act" if by_act(prev % PER) else "dve"
            pe.wait_ge(read_act if engine == "act" else read_dve, count(n, prev, engine))

        block = ctx.enter_context(nc.Block())

        @block.sync
        def _(sp):
            def head(i, p):
                n = i * 2 + p
                if real(n, 2):
                    sp.wait_ge(scores_ready, QT * n - QT)
                for r in range(2):
                    rows = slice(2 * DK * r, 2 * DK * (r + 1))
                    sp.dma_start(q_parts[rows, p], bass.AP(scratch["q"], n * HEAD, [[NH * HEAD, 2], [S, DK], [1, S]])
                                 ).then_inc(q_loaded[p], DMA)
                    sp.dma_start(k_parts[rows, p], bass.AP(scratch["k"], r * NH * HEAD + n * HEAD,
                                                           [[0, 2], [S, DK], [1, S]])).then_inc(k_loaded[p], DMA)
                if real(n, 2):
                    sp.wait_ge(bias_done, QT * n - QT)
                sp.dma_start(skew[:, p], bass.AP(scratch["rel"].tensor, n * s.REL + 1, [[1, P], [1, s.SKEW]])
                             ).then_inc(skew_loaded[p], DMA)
                if real(n, 2):
                    sp.wait_ge(values_ready, n - 1)
                sp.dma_start(v_head[:, p], bass.AP(scratch["v"], n * S * DK, [[DK, P], [P * DK, QT], [1, DK]])
                             ).then_inc(v_loaded[p], DMA)
            loops(sp, head, False)

        @block.gpsimd
        def _(pool):
            all_kept = pool.value_load(keep["all_kept"][0:1, 0:1])
            pool.sem_inc(o_low, 1)

            def store_head(i, p, wait_stored):
                m = i * 2 + p
                pool.wait_ge(o_ready, m + 2)
                if wait_stored and real(m, 2):
                    pool.wait_ge(o_stored[p], i * 2 * DMA)
                settle(pool, pool_gate)
                pool.tensor_copy(o_cut[:, p, HI], o_head[:, p]).then_inc(o_high, 1)
                pool.wait_ge(o_high, m + 1)
                pool.tensor_tensor(o_cut[:, p, LO], o_head[:, p], o_cut[:, p, HI], ALU.subtract).then_inc(o_low, 1)
                pool.wait_ge(o_low, m + 2)
                for part in (HI, LO):
                    pool.dma_start(bass.AP(scratch["o"], part * NH * HEAD + m * HEAD, [[QC, CHUNKS], [S, DK], [1, QC]]),
                                   o_cut[:, p, part]).then_inc(o_stored[p], DMA)

            def penalties(i, p, t):
                n = i * 2 + p
                slot = t % 2
                if real(n, 1) or t >= 2:
                    pool.wait_ge(scores_ready, QT * n + t - 1)
                rows = (n // s.H) * (S * S) + t * P * S
                pool.dma_start(mask_u[:, slot], bass.AP(io["mask"].tensor, rows, [[S, P], [1, S]])
                               ).then_inc(mask_in[slot], DMA)
                pool.wait_ge(mask_in[slot], (n * (QT // 2) + t // 2 + 1) * DMA)
                settle(pool, pool_gate)
                pool.tensor_scalar(penalty[:, slot], mask_u[:, slot], -MASKED, MASKED, ALU.mult, ALU.add
                                   ).then_inc(penalty_ready, 1)

            with pool.If(all_kept == 1):
                for p in range(2):
                    store_head(0, p, True)
                with pool.Fori(1, NH // 2) as i:
                    for p in range(2):
                        store_head(i, p, True)
            with pool.Else():
                def head(i, p):
                    for t in range(QT):
                        if real(i * 2 + p):
                            penalties(i, p, t)
                        if t == 5 and real(i * 2 + p, 2):
                            store_head(i - 1, p, False)
                        if t == QT - 1 and real(i * 2 + p, 2):
                            pool.wait_ge(o_stored[p], i * 2 * DMA)
                loops(pool, head, True)
            for p in range(2):
                pool.wait_ge(o_stored[p], NH * DMA)

        @block.vector
        def _(dve):
            dve.sem_inc(o_ready, 1)

            def head(i, p):
                n = i * 2 + p
                for t in range(QT):
                    if t == LAG and real(n, 2):
                        dve.wait_ge(values_ready, n - 1)
                        dve.wait_ge(read_act, count(n, spread_idx - PER, "act"))
                        dve.wait_ge(o_low, n - 1)
                        dve.scalar_tensor_tensor(out=o_head[:, p], in0=values, scalar=OUT_SCALE, in1=spread[:, p],
                                                 op0=ALU.mult, op1=ALU.mult).then_inc(o_ready, 1)
                    if real(n):
                        if t == 0:
                            dve.wait_ge(skew_loaded[p], (i + 1) * DMA)
                        dve.wait_ge(scores_ready, QT * n + t + 1)
                        if real(n, 1) or t >= 4:
                            dve.wait_ge(probs_ready, QT * n + t - 3)
                        settle(dve, dve_gate)
                        col = p * QT + t
                        at = S - P - t * P
                        dve.tensor_tensor_reduce(
                            out=biased[:, t % 4], in0=ps[:, 2 * (t % 2):2 * (t % 2) + 2].rearrange("p b k -> p (b k)"),
                            in1=skew[:, p, at:at + S], scale=-1 / SCORE_SCALE, scalar=3e38, op0=ALU.add, op1=ALU.min,
                            accum_out=neg_max[:, col:col + 1]).then_inc(bias_done, 1)
                    if t == 2 and real(n, 1):
                        dve.wait_ge(probs_ready, QT * n)
                        dve.reciprocal(recip[:, 1 - p], row_sum[:, 1 - p]).then_inc(recip_done, 1)
                    for idx in range(first_item[t], PER if t == QT - 1 else first_item[t + 1]):
                        kind, _, h = items[idx]
                        if by_act(idx) or not item_exists_at(n, idx):
                            continue
                        m_par = p if t >= LAG else 1 - p
                        unit = (t - LAG) % QT
                        dve.wait_ge(item_ready, count(n, idx))
                        if unit == 0 and real(n, 2):
                            dve.wait_ge(values_ready, n - 1)
                        dve.tensor_copy(probs_T[:, m_par, 4 * h:4 * h + 4, unit * P:(unit + 1) * P],
                                        ps[:, 4 + idx % T_BANKS].rearrange("p (k q) -> p k q", q=P)
                                        ).then_inc(read_dve, 1)
            loops(dve, head, True)

        @block.scalar
        def _(act):
            def head(i, p):
                n = i * 2 + p
                for t in range(QT):
                    if real(n, 1 if t == 0 else 0):
                        unit, par = (t - 1) % QT, p if t > 0 else 1 - p
                        col = par * QT + unit
                        act.wait_ge(bias_done, QT * n + t)
                        if real(n, 1) or t >= 5:
                            last = first_item[(t - 2) % QT] + 1 - (PER if t < 2 else 0)
                            act.wait_ge(item_ready, count(n, last))
                        if t == 1 and real(n, 2):
                            act.wait_ge(recip_done, n - 1)
                        act.activation(probs[:, unit % 4], biased[:, unit % 4], ACT.Exp, bias=neg_max[:, col:col + 1],
                                       scale=-1.0, accum_out=row_sum[:, par, unit:unit + 1]).then_inc(probs_ready, 1)
                    for idx in range(first_item[t], PER if t == QT - 1 else first_item[t + 1]):
                        kind, _, h = items[idx]
                        if not by_act(idx) or not item_exists_at(n, idx):
                            continue
                        bank = ps[:, 4 + idx % T_BANKS]
                        act.wait_ge(item_ready, count(n, idx))
                        if kind == "half":
                            m_par = p if t >= LAG else 1 - p
                            unit = (t - LAG) % QT
                            if unit == 0 and real(n, 2):
                                act.wait_ge(values_ready, n - 1)
                            act.copy(probs_T[:, m_par, 4 * h:4 * h + 4, unit * P:(unit + 1) * P],
                                     bank.rearrange("p (k q) -> p k q", q=P)).then_inc(read_act, 1)
                        elif kind == "sums":
                            act.copy(recip_T[:], bank[0:QT, 0:P]).then_inc(read_act, 1)
                        else:
                            if real(n, 2):
                                act.wait_ge(o_ready, n - 1)
                            act.copy(spread[:, 1 - p], bank[:, 0:QC]).then_inc(read_act, 1)
            loops(act, head, True)

        @block.tensor
        def _(pe):
            exchange, exchange_b, select = keep["exchange"], keep["exchange_b"], keep["select"]
            all_kept = pe.value_load(keep["all_kept"][0:1, 0:1])

            def weighted_values(i_of, par, n, kt):
                if kt == 0:
                    pe.wait_ge(v_loaded[par], (i_of + 1) * DMA)
                    for name, sem_ in (("act", read_act), ("dve", read_dve)):
                        pe.wait_ge(sem_, count(n, first_item[LAG] - 1, name))
                    if real(n, 2):
                        pe.wait_ge(o_ready, n)
                for c in range(CHUNKS):
                    ins = pe.matmul(values[c * DK:(c + 1) * DK], v_head[:, par, kt],
                                    probs_T[:, par, kt, c * QC:(c + 1) * QC],
                                    start=(kt == 0), stop=(kt == QT - 1))
                if kt == QT - 1:
                    ins.then_inc(values_ready, 1)

            def head(i, p, masked):
                n = i * 2 + p
                for t in range(QT):
                    slot = t % 2
                    if real(n):
                        if t == 0:
                            pe.wait_ge(q_loaded[p], (i + 1) * 2 * DMA)
                            pe.wait_ge(k_loaded[p], (i + 1) * 2 * DMA)
                        if real(n, 1) or t >= 2:
                            pe.wait_ge(bias_done, QT * n + t - 1)
                        if masked:
                            pe.wait_ge(penalty_ready, QT * n + t + 1)
                        for k in range(S // 512):
                            bank = ps[:, 2 * slot + k]
                            ins = pe.matmul(bank, q_parts[:, p, t * P:(t + 1) * P],
                                            k_parts[:, p, k * 512:(k + 1) * 512], start=True, stop=not masked)
                            if masked:
                                ins = pe.matmul(bank, exchange_b[:], penalty[:, slot, k * 512:(k + 1) * 512],
                                                start=False, stop=True)
                        ins.then_inc(scores_ready, 1)
                    for idx in range(first_item[t], PER if t == QT - 1 else first_item[t + 1]):
                        kind, _, h = items[idx]
                        if not item_exists_at(n, idx):
                            continue
                        bank = ps[:, 4 + idx % T_BANKS]
                        wait_read(pe, n, idx)
                        if kind == "half":
                            if h == 0:
                                pe.wait_ge(probs_ready, QT * n + t - LAG + 1)
                            for k in range(4):
                                kt = 4 * h + k
                                ins = pe.transpose(bank[:, k * P:(k + 1) * P],
                                                   probs[:, (t - LAG) % 4, kt * P:(kt + 1) * P], exchange[:])
                        elif kind == "sums":
                            pe.wait_ge(recip_done, n)
                            ins = pe.transpose(bank[0:QT, 0:P], recip[:, 1 - p], exchange[:])
                        else:
                            pe.wait_ge(read_act, count(n, sums_idx, "act"))
                            for u in range(2):
                                ins = pe.matmul(bank[:, u * P:(u + 1) * P],
                                                select[:, u].rearrange("r c d -> r (c d)"), recip_T[:],
                                                start=True, stop=True)
                        ins.then_inc(item_ready, 1)
                    if t in VALUES_NEXT and real(n, 1):
                        weighted_values(i if p == 1 else i - 1, 1 - p, n, VALUES_NEXT[t])
                    if t in VALUES_AFTER and real(n, 2):
                        weighted_values(i - 1, p, n, VALUES_AFTER[t])

            with pe.If(all_kept == 1):
                loops(pe, lambda i, p: head(i, p, False), True)
            with pe.Else():
                loops(pe, lambda i, p: head(i, p, True), True)


def feed_phase(nc, s, io, scratch, keep):
    KT, TT, CH, D, FT, E = s.KT, s.TT, s.CH, s.D, s.FT, s.E
    PAIRS = FT // 2
    STAGES = 4
    half = s.S // CH
    with ExitStack() as ctx:
        sb = lambda name, shape, dt: ctx.enter_context(nc.sbuf_tensor(name, shape, dt))
        sem = lambda name: ctx.enter_context(nc.semaphore(name))
        w_raw = sb("ffn_raw", [P, STAGES, 2, 1024], F32)
        w1c = sb("w1_cut", [P, PAIRS, 2, KT, 2 * P], F16)
        w2c = sb("w2_cut", [P, PAIRS, 2, 2, D], F16)
        o_in = sb("o_in", [P, 2, KT, CH], F16)
        x_in = sb("x_res", [P, TT, D], F32)
        b2_row = sb("b2_row", [P, D], F32)
        x_new = sb("x_new", [P, TT, D], F32)
        x_cur = sb("x_cur", [P, TT, D], F32)
        stats = sb("stats2", [P, TT, 6], F32)
        moments = sb("moments2", [P, TT, 2], F32)
        var_eps = sb("var_eps2", [P, TT], F32)
        rstd = sb("rstd2", [P, TT], F32)
        minus_half = sb("minus_half2", [P, TT], F32)
        x_norm = sb("x_norm2", [P, TT, D], F32)
        xT = sb("xT2", [P, 2, KT, CH], F16)
        hidden = sb("hidden", [P, 4, CH], F32)
        h_cut = sb("h_cut", [P, 4, 2, CH], F16)
        y_out = sb("y_out", [P, TT, D], F32)
        ps = ctx.enter_context(nc.psum_tensor("ps_feed", [P, 8, 512], F32))

        raw_loaded = [sem(f"raw_loaded{k}") for k in range(STAGES)]
        w_high, w_low = sem("w_high"), sem("w_low")
        o_loaded, x_loaded, b2_loaded = sem("o_loaded"), sem("x_res_loaded"), sem("b2_loaded")
        half_ready = sem("half_ready")
        pool_gate, dve_gate = sem("pool_gate3"), sem("dve_gate3")
        projected = sem("projected")
        x_new_done, x_cur_done = sem("x_new_done"), sem("x_cur_done")
        stats_done, moments_done, normed = sem("stats2_done"), sem("moments2_done"), sem("x2_normed")
        var_done, rstd_done = sem("var2_done"), sem("rstd2_done")
        turned, turned_hi, turned_lo = sem("turned2"), sem("turned2_hi"), sem("turned2_lo")
        hidden_ready = sem("hidden_ready")
        gelu_done = sem("gelu_done")
        h_high, h_low = sem("h_high"), sem("h_low")
        slice_used = sem("slice_used")
        y_done = sem("y_done")
        y_stored = sem("y_stored")

        x_rows = io["x"].rearrange("b s d -> (b s) d").rearrange("(c t p) d -> c p t d", t=TT, p=P)
        out_rows = io["out"].rearrange("b s d -> (b s) d").rearrange("(c t p) d -> c p t d", t=TT, p=P)
        STEPS = FT + 2
        PROJECT_AT = {3: 0, 5: 1, 7: 2, 9: 3}
        NORM_AT = 12
        TURN_AT = {FT - 1: [0, 1], FT: [2, 3]}
        CUT_AT = {2 * k + 4: k for k in range(PAIRS - 1)}

        block = ctx.enter_context(nc.Block())

        def load_tokens(eng, e):
            eng.dma_start(x_in[:], x_rows[e]).then_inc(x_loaded, DMA)
            for part in (HI, LO):
                eng.dma_start(o_in[:, part], bass.AP(
                    scratch["o"], part * s.T * D + (e // half) * (D * s.S) + (e % half) * CH,
                    [[s.S, P], [P * s.S, KT], [1, CH]])).then_inc(o_loaded, DMA)

        @block.sync
        def _(sp):
            def load_pair(e, k):
                slot = k % STAGES
                if later(e) or k >= STAGES:
                    done = (e * PAIRS + k - STAGES + 1) * 2
                    sp.wait_ge(w_high, done)
                    sp.wait_ge(w_low, done)
                sp.dma_start(w_raw[:, slot, 0].rearrange("p (k f) -> p k f", k=KT),
                             bass.AP(io["w1"].tensor, e * D * s.F + k * 2 * P, [[s.F, P], [P * s.F, KT], [1, 2 * P]])
                             ).then_inc(raw_loaded[slot], DMA)
                sp.dma_start(w_raw[:, slot, 1].rearrange("p (f d) -> p f d", f=2),
                             bass.AP(io["w2"].tensor, e * D * s.F + k * 2 * P * D, [[D, P], [P * D, 2], [1, D]])
                             ).then_inc(raw_loaded[slot], DMA)
            for k in range(PAIRS):
                load_pair(0, k)
            with sp.Fori(1, E) as e:
                for k in range(PAIRS):
                    load_pair(e, k)

        @block.gpsimd
        def _(pool):
            pool.memset(minus_half[:], -0.5).then_inc(half_ready, 1)
            pool.wait_ge(half_ready, 1)
            load_tokens(pool, 0)

            def rstd_of(e):
                pool.wait_ge(moments_done, e + 1)
                settle(pool, pool_gate)
                pool.tensor_scalar(var_eps[:], moments[:, :, 1], 1.0, EPS, ALU.mult, ALU.add).then_inc(var_done, 1)
                pool.wait_ge(var_done, e + 1)
                pool.tensor_tensor(rstd[:], var_eps[:], minus_half[:], ALU.pow).then_inc(rstd_done, 1)

            def load_b2(e):
                if later(e):
                    pool.wait_ge(x_cur_done, e * TT)
                pool.dma_start(b2_row[:], bass.AP(io["b2"].tensor, e * D, [[0, P], [1, D]])).then_inc(b2_loaded, DMA)

            def load_next(e):
                pool.wait_ge(projected, e * TT)
                pool.wait_ge(x_new_done, e * TT)
                load_tokens(pool, e)

            def store(e):
                pool.wait_ge(y_done, (e + 1) * TT)
                pool.dma_start(out_rows[e], y_out[:]).then_inc(y_stored, DMA)

            load_b2(0)
            rstd_of(0)
            load_next(1)
            load_b2(1)
            rstd_of(1)
            with pool.Fori(1, E - 1) as e:
                load_next(e + 1)
                store(e - 1)
                load_b2(e + 1)
                rstd_of(e + 1)
            store(E - 2)
            store(E - 1)
            pool.wait_ge(y_stored, E * DMA)

        @block.scalar
        def _(act):
            def cut_high(e, k):
                slot = k % STAGES
                act.wait_ge(raw_loaded[slot], (e * (PAIRS // STAGES) + k // STAGES + 1) * 2 * DMA)
                if later(e):
                    act.wait_ge(slice_used, (e - 1) * FT + 2 * k + 2)
                act.activation(w1c[:, k, HI], w_raw[:, slot, 0].rearrange("p (k f) -> p k f", k=KT), ACT.Copy,
                               scale=WEIGHT_SCALE).then_inc(w_high, 1)
                act.activation(w2c[:, k, HI], w_raw[:, slot, 1].rearrange("p (f d) -> p f d", f=2), ACT.Copy,
                               scale=WEIGHT_SCALE).then_inc(w_high, 1)

            def turned_high(e, kt):
                act.wait_ge(turned, e * KT + kt + 1)
                act.copy(xT[:, HI, kt], ps[:, 6 + kt % 2]).then_inc(turned_hi, 1)

            def frame(e, more):
                for f in range(STEPS):
                    if f < FT:
                        act.wait_ge(hidden_ready, e * FT + f + 1)
                        if f >= 4:
                            act.wait_ge(h_low, e * FT + f - 3)
                        elif later(e):
                            act.wait_ge(h_low, e * FT)
                        bias = keep["b1T"][:, bass.ds(e * FT + f, 1)]
                        act.activation(hidden[:, f % 4], ps[:, 4 + f % 2], ACT.Gelu_apprx_tanh, bias=bias,
                                       scale=1 / WEIGHT_SCALE).then_inc(gelu_done, 1)
                    if f == 1:
                        cut_high(e, PAIRS - 1)
                    if more and f in CUT_AT:
                        cut_high(e + 1, CUT_AT[f])
                    if more and f in TURN_AT:
                        for kt in TURN_AT[f]:
                            turned_high(e + 1, kt)

            for k in range(PAIRS - 1):
                cut_high(0, k)
            for kt in range(KT):
                turned_high(0, kt)
            frame(0, True)
            with act.Fori(1, E - 1) as e:
                frame(e, True)
            frame(E - 1, False)

        @block.vector
        def _(dve):
            def cut_low(e, k):
                slot = k % STAGES
                done = (e * PAIRS + k) * 2
                dve.wait_ge(w_high, done + 1)
                dve.scalar_tensor_tensor(out=w1c[:, k, LO], in0=w_raw[:, slot, 0].rearrange("p (k f) -> p k f", k=KT),
                                         scalar=WEIGHT_SCALE, in1=w1c[:, k, HI], op0=ALU.mult, op1=ALU.subtract
                                         ).then_inc(w_low, 1)
                dve.wait_ge(w_high, done + 2)
                dve.scalar_tensor_tensor(out=w2c[:, k, LO], in0=w_raw[:, slot, 1].rearrange("p (f d) -> p f d", f=2),
                                         scalar=WEIGHT_SCALE, in1=w2c[:, k, HI], op0=ALU.mult, op1=ALU.subtract
                                         ).then_inc(w_low, 1)

            def residual(e, t):
                if t == 0:
                    dve.wait_ge(x_loaded, (e + 1) * DMA)
                dve.wait_ge(projected, e * TT + t + 1)
                dve.scalar_tensor_tensor(out=x_new[:, t], in0=ps[:, 6 + t % 2], scalar=1 / (WEIGHT_SCALE * OUT_SCALE),
                                         in1=x_in[:, t], op0=ALU.mult, op1=ALU.add).then_inc(x_new_done, 1)
                dve.wait_ge(x_new_done, e * TT + t + 1)
                dve.bn_stats(stats[:, t], x_new[:, t]).then_inc(stats_done, 1)

            def aggregate(e):
                dve.wait_ge(stats_done, (e + 1) * TT)
                settle(dve, dve_gate)
                for t in range(TT):
                    ins = dve.bn_aggr(moments[:, t], stats[:, t])
                ins.then_inc(moments_done, 1)

            def normalize(e):
                dve.wait_ge(rstd_done, e + 1)
                for t in range(TT):
                    dve.tensor_scalar(x_norm[:, t], x_new[:, t], moments[:, t, 0:1], rstd[:, t:t + 1],
                                      ALU.subtract, ALU.mult).then_inc(normed, 1)

            def turned_low(e, kt):
                dve.wait_ge(turned_hi, e * KT + kt + 1)
                dve.tensor_tensor(xT[:, LO, kt], ps[:, 6 + kt % 2], xT[:, HI, kt], ALU.subtract).then_inc(turned_lo, 1)

            def add_b2(e):
                dve.wait_ge(b2_loaded, (e + 1) * DMA)
                if later(e):
                    dve.wait_ge(y_done, e * TT)
                for t in range(TT):
                    dve.tensor_tensor(x_cur[:, t], x_new[:, t], b2_row[:], ALU.add).then_inc(x_cur_done, 1)

            def output(e):
                dve.wait_ge(slice_used, (e + 1) * FT)
                if later(e):
                    dve.wait_ge(y_stored, e * DMA)
                dve.wait_ge(x_cur_done, (e + 1) * TT)
                for t in range(TT):
                    dve.scalar_tensor_tensor(out=y_out[:, t], in0=ps[:, t], scalar=1 / WEIGHT_SCALE, in1=x_cur[:, t],
                                             op0=ALU.mult, op1=ALU.add).then_inc(y_done, 1)

            def frame(e, more):
                for f in range(STEPS):
                    if f == 1:
                        cut_low(e, PAIRS - 1)
                    if f < FT:
                        dve.wait_ge(gelu_done, e * FT + f + 1)
                        if f >= 4:
                            dve.wait_ge(slice_used, e * FT + f - 3)
                        elif later(e):
                            dve.wait_ge(slice_used, e * FT)
                        dve.tensor_copy(h_cut[:, f % 4, HI], hidden[:, f % 4]).then_inc(h_high, 1)
                        dve.wait_ge(h_high, e * FT + f + 1)
                        dve.tensor_tensor(h_cut[:, f % 4, LO], hidden[:, f % 4], h_cut[:, f % 4, HI],
                                          ALU.subtract).then_inc(h_low, 1)
                    if more and f in CUT_AT:
                        cut_low(e + 1, CUT_AT[f])
                    if more and f in PROJECT_AT:
                        residual(e + 1, PROJECT_AT[f])
                    if more and f == 9:
                        aggregate(e + 1)
                    if more and f == NORM_AT:
                        normalize(e + 1)
                    if more and f in TURN_AT:
                        for kt in TURN_AT[f]:
                            turned_low(e + 1, kt)
                output(e)
                if more:
                    add_b2(e + 1)

            for k in range(PAIRS - 1):
                cut_low(0, k)
            for t in range(TT):
                residual(0, t)
            aggregate(0)
            normalize(0)
            for kt in range(KT):
                turned_low(0, kt)
            add_b2(0)
            frame(0, True)
            with dve.Fori(1, E - 1) as e:
                frame(e, True)
            frame(E - 1, False)

        @block.tensor
        def _(pe):
            woT, ident = keep["woT"], keep["ident"]
            last_pass = len(PASSES) - 1

            def project(e, t):
                if t == 0:
                    pe.wait_ge(o_loaded, (e + 1) * 2 * DMA)
                if t < 2:
                    if later(e):
                        pe.wait_ge(turned_lo, e * KT)
                else:
                    pe.wait_ge(x_new_done, e * TT + t - 1)
                steps = [(kt, a, b) for kt in range(KT) for a, b in PASSES]
                for n, (kt, a, b) in enumerate(steps):
                    ins = pe.matmul(ps[:, 6 + t % 2], o_in[:, a, kt, t * P:(t + 1) * P], woT[:, b, kt],
                                    start=(n == 0), stop=(n == len(steps) - 1))
                ins.then_inc(projected, 1)

            def turn(e, kt):
                if kt == 0:
                    pe.wait_ge(normed, (e + 1) * TT)
                if kt < 2:
                    pe.wait_ge(x_new_done, e * TT + 3 + kt)
                else:
                    pe.wait_ge(turned_lo, e * KT + kt - 1)
                for t in range(TT):
                    ins = pe.transpose(ps[:, 6 + kt % 2, t * P:(t + 1) * P], x_norm[:, t, kt * P:(kt + 1) * P], ident[:])
                ins.then_inc(turned, 1)

            def first(e, f):
                if f == 0:
                    pe.wait_ge(turned_lo, (e + 1) * KT)
                if f % 2 == 0:
                    pe.wait_ge(w_low, (e * PAIRS + f // 2 + 1) * 2)
                if later(e) or f >= 2:
                    pe.wait_ge(gelu_done, e * FT + (f - 1 if f >= 2 else 0))
                steps = [(kt, a, b) for kt in range(KT) for a, b in PASSES]
                for n, (kt, a, b) in enumerate(steps):
                    ins = pe.matmul(ps[:, 4 + f % 2], w1c[:, f // 2, a, kt, (f % 2) * P:(f % 2 + 1) * P], xT[:, b, kt],
                                    start=(n == 0), stop=(n == len(steps) - 1))
                ins.then_inc(hidden_ready, 1)

            def second(e, f):
                pe.wait_ge(h_low, e * FT + f + 1)
                if f == 0 and later(e):
                    pe.wait_ge(y_done, e * TT)
                for t in range(TT):
                    for n, (a, b) in enumerate(PASSES):
                        ins = pe.matmul(ps[:, t], h_cut[:, f % 4, a, t * P:(t + 1) * P], w2c[:, f // 2, b, f % 2],
                                        start=(f == 0 and n == 0), stop=(f == FT - 1 and n == last_pass))
                ins.then_inc(slice_used, 1)

            def frame(e, more):
                for f in range(STEPS):
                    if f < FT:
                        first(e, f)
                    if more and f in PROJECT_AT:
                        project(e + 1, PROJECT_AT[f])
                    if more and f in TURN_AT:
                        for kt in TURN_AT[f]:
                            turn(e + 1, kt)
                    if f >= 2:
                        second(e, f - 2)

            for t in range(TT):
                project(0, t)
            for kt in range(KT):
                turn(0, kt)
            frame(0, True)
            with pe.Fori(1, E - 1) as e:
                frame(e, True)
            frame(E - 1, False)


def build(nc, io):
    s = Shapes(io["x"], io["rel_emb"], io["w1"])
    scratch = {
        "q": nc.dram_tensor("q_scratch", [2, s.NH * s.DK, s.S], F16),
        "k": nc.dram_tensor("k_scratch", [2, s.NH * s.DK, s.S], F16),
        "v": nc.dram_tensor("v_scratch", [s.NH, s.S, s.DK], F32),
        "o": nc.dram_tensor("o_scratch", [2, s.NH * s.DK, s.S], F16),
        "rel": nc.dram_tensor("rel_scratch", [s.NH, s.REL], F32).ap(),
    }
    with ExitStack() as ctx:
        sb = lambda name, shape, dt: ctx.enter_context(nc.sbuf_tensor(name, shape, dt))
        keep = {
            "ident": sb("ident", [P, P], F32),
            "exchange": sb("exchange", [P, P], F32),
            "exchange_b": sb("exchange_b", [P, P], BF16),
            "select": sb("select", [s.QT, 2, 4, s.DK], F32),
            "woT": sb("woT", [P, 2, s.KT, s.D], F16),
            "b1T": sb("b1T", [P, s.E * s.FT], F32),
            "all_kept": sb("all_kept", [1, 1], I32),
        }
        project_phase(nc, s, io, scratch, keep)
        attend_phase(nc, s, io, scratch, keep)
        feed_phase(nc, s, io, scratch, keep)


_NAMES = {
    "x": "x", "ctx": "ctx_1024", "mask": "mask_Bx1xSxS2_bf1", "wq": "L0_xattn_w_q", "wk": "L0_xattn_w_k",
    "wv": "L0_xattn_w_v", "wo": "L0_xattn_w_o", "rel_emb": "L0_xattn_rel_emb", "w1": "L0_ffn_w1",
    "b1": "L0_ffn_b1", "w2": "L0_ffn_w2", "b2": "L0_ffn_b2",
}


def kernel(**inputs):
    import numpy as np
    import concourse.bacc as bacc
    from concourse.bass_utils import run_bass_kernel_spmd

    nc = bacc.Bacc("TRN2", target_bir_lowering=False, num_devices=1)
    arrays, io = {}, {}
    for short, name in _NAMES.items():
        a = np.ascontiguousarray(inputs[name])
        if a.dtype == bool:
            a = a.view(np.uint8)
        arrays[f"in_{short}"] = a
        io[short] = nc.dram_tensor(f"in_{short}", a.shape, mybir.dt.from_np(a.dtype), kind="ExternalInput").ap()
    io["out"] = nc.dram_tensor("out_0", inputs["x"].shape, F32, kind="ExternalOutput").ap()
    build(nc, io)
    r = run_bass_kernel_spmd(nc, [arrays], core_ids=[0])
    return r.results[0]["out_0"]
```

```python
from contextlib import ExitStack

import concourse.bass as bass
from concourse import mybir

ALU = mybir.AluOpType
ACT = mybir.ActivationFunctionType
AXIS = mybir.AxisListType
F32 = mybir.dt.float32
F16 = mybir.dt.float16
BF16 = mybir.dt.bfloat16
I32 = mybir.dt.int32
U8 = mybir.dt.uint8

P = 128
DMA = 16
HI, LO = 0, 1
EPS = 1e-5

WEIGHT_SCALE = 64.0
RECIP_SCALE = 1024.0
OUT_SCALE = 16.0
SCORE_SCALE = 4.0
MASKED = -(2.0**100)


class Shapes:
    def __init__(self, x, rel_emb, w1):
        self.B, self.S, self.D = x.shape
        self.H = rel_emb.shape[1]
        self.DK = self.D // self.H
        self.E, _, self.F = w1.shape
        self.T = self.B * self.S
        self.KT = self.D // P
        self.CH = 512
        self.NCH = self.T // self.CH
        self.TT = self.CH // P
        self.HG = P // self.DK
        self.NH = self.B * self.H
        self.QT = self.S // P
        self.REL = 2 * self.S
        self.SKEW = self.S + self.S - P
        self.FT = self.F // P
        self.STAGES = 4
        assert self.DK == 32 and self.CH == self.T // self.E and self.D == 512 and self.S % self.CH == 0


PASSES = [(HI, HI), (HI, LO), (LO, HI)]


def later(c):
    return not isinstance(c, int) or c > 0


def settle(eng, gate):
    eng.sem_inc(gate, 1)


def project_phase(nc, s, io, scratch, keep):
    KT, TT, CH, D, NCH, QT = s.KT, s.TT, s.CH, s.D, s.NCH, s.QT
    with ExitStack() as ctx:
        sb = lambda name, shape, dt: ctx.enter_context(nc.sbuf_tensor(name, shape, dt))
        sem = lambda name: ctx.enter_context(nc.semaphore(name))
        w_raw = keep["weights_in"].rearrange("p w (k d) -> p w k d", k=KT)
        wT = sb("wT", [P, 3, 2, KT, D], F16)
        rel_raw = sb("rel_raw", [P, s.REL // P, s.H], F32)
        rel_rev = sb("rel_rev", [s.H, s.REL], F32)
        b1_raw = sb("b1_raw", [s.E * s.FT, P], F32)
        x_in = sb("x_in", [P, TT, D], F32)
        c_in = sb("c_in", [P, TT, D], F32)
        m_in = sb("m_in", [P, TT, s.S], U8)
        stats = sb("stats", [P, TT, 6], F32)
        moments = sb("moments", [P, TT, 2], F32)
        var_eps = sb("var_eps", [P, TT], F32)
        rstd = sb("rstd", [P, TT], F32)
        minus_half = sb("minus_half", [P, TT], F32)
        x_norm = sb("x_norm", [P, TT, D], F32)
        xT = sb("xT", [P, 2, KT, CH], F16)
        cT = sb("cT", [P, 2, KT, CH], F16)
        qk_cut, q_stored = keep["qk_cut"], keep["q_stored"]
        v_out = sb("v_out", [P, 4, D], F32)
        m_new = sb("m_new", [P, 1], F32)
        m_min = sb("m_min", [P, 1], F32)
        ps = ctx.enter_context(nc.psum_tensor("ps_project", [P, 8, 512], F32))

        w_loaded = [sem(f"{name}_loaded") for name in ("wq", "wk", "wv", "wo")]
        b1_loaded, rel_loaded = sem("b1_loaded"), sem("rel_loaded")
        x_loaded, c_loaded, m_loaded = sem("x_loaded"), sem("c_loaded"), sem("m_loaded")
        consts_ready = sem("consts_ready")
        turned = sem("turned")
        turned_hi, turned_lo = sem("turned_hi"), sem("turned_lo")
        multiplied = sem("multiplied")
        product_hi, product_lo = sem("product_hi"), sem("product_lo")
        pool_gate, dve_gate = keep["pool_gate"], sem("dve_gate")
        stats_done, moments_done = sem("stats_done"), sem("moments_done")
        var_done, rstd_done = sem("var_done"), sem("rstd_done")
        x_normed, mask_read, mask_min_done = sem("x_normed"), sem("mask_read"), sem("mask_min_done")
        b1_turned, b1_kept = sem("b1_turned"), sem("b1_kept")
        rel_rev_stored, k_stored, v_stored = sem("rel_rev_stored"), sem("k_stored"), sem("v_stored")
        flag_turned, flag_kept, rel_zeroed = sem("flag_turned"), sem("flag_kept"), sem("rel_zeroed")

        T_BANKS = M_BANKS = 4
        W_ITEMS = 4 * KT
        REL_ITEMS = s.REL // 512
        SETUP = W_ITEMS + REL_ITEMS
        assert SETUP % T_BANKS == 0
        T_CHUNK = 2 * KT
        M_CHUNK = 3 * TT
        FIRST = {"wk": 0, "ctx": KT, "wv": 2 * KT, "x": 3 * KT, "wq": 4 * KT, "wo": 5 * KT, "rel": 6 * KT}
        W_INDEX = {"wq": 0, "wk": 1, "wv": 2, "wo": 3}

        def ctx_item(c):
            return SETUP + c * T_CHUNK if later(c) else FIRST["ctx"]

        def x_item(c):
            return SETUP + c * T_CHUNK + KT if later(c) else FIRST["x"]

        def low_item(c, item):
            return item - REL_ITEMS if later(c) else item

        weight_src = [io["wq"], io["wk"], io["wv"], io["wo"]]
        chunk_rows = "(c t p) d -> c p t d"
        x_rows = io["x"].rearrange("b s d -> (b s) d").rearrange(chunk_rows, t=TT, p=P)
        ctx_rows = io["ctx"].rearrange("b s d -> (b s) d").rearrange(chunk_rows, t=TT, p=P)
        mask_rows = io["mask"].rearrange("b o q k -> (b o q) k").rearrange(chunk_rows, t=TT, p=P)

        def wT_of(w, part):
            return keep["woT"][:, part] if w == 3 else wT[:, w, part]

        block = ctx.enter_context(nc.Block())

        @block.gpsimd
        def _(pool):
            ident, exchange, select = keep["ident"], keep["exchange"], keep["select"]
            pool.memset(ident[:], 0.0).then_inc(consts_ready, 1)
            pool.memset(exchange[:], 0.0).then_inc(consts_ready, 1)
            pool.memset(select[:], 0.0).then_inc(consts_ready, 1)
            pool.memset(minus_half[:], -0.5).then_inc(consts_ready, 1)
            pool.wait_ge(consts_ready, 4)
            pool.affine_select(out=ident[:], in_=ident[:], compare_op=ALU.not_equal, fill=1.0, base=0,
                               pattern=[[-1, P]], channel_multiplier=1).then_inc(consts_ready, 1)
            pool.affine_select(out=exchange[:], in_=exchange[:], compare_op=ALU.not_equal, fill=1.0,
                               base=-(P - 1), pattern=[[1, P]], channel_multiplier=1).then_inc(consts_ready, 1)
            for n, part in enumerate((HI, LO)):
                pool.wait_ge(consts_ready, 6 + n)
                pool.affine_select(out=select[:], in_=select[:], compare_op=ALU.not_equal, fill=1.0, base=-part * QT,
                                   pattern=[[-1, 2], [-2, 4], [0, s.DK]], channel_multiplier=1).then_inc(consts_ready, 1)
            pool.wait_ge(consts_ready, 8)
            pool.tensor_copy(keep["exchange_b"][:], exchange[:]).then_inc(consts_ready, 1)
            pool.tensor_copy(keep["exchange_h"][:], exchange[:]).then_inc(consts_ready, 1)

            def chunk(c):
                if later(c):
                    pool.wait_ge(x_normed, c * TT)
                pool.dma_start(x_in[:], x_rows[c]).then_inc(x_loaded, DMA)
                pool.wait_ge(moments_done, c + 1)
                settle(pool, pool_gate)
                pool.tensor_scalar(var_eps[:], moments[:, :, 1], 1.0, EPS, ALU.mult, ALU.add).then_inc(var_done, 1)
                pool.wait_ge(var_done, c + 1)
                pool.tensor_tensor(rstd[:], var_eps[:], minus_half[:], ALU.pow).then_inc(rstd_done, 1)
                if later(c):
                    pool.wait_ge(mask_read, c)
                pool.dma_start(m_in[:], mask_rows[c]).then_inc(m_loaded, DMA)

            chunk(0)
            with pool.Fori(1, NCH) as c:
                chunk(c)

        @block.scalar
        def _(act):
            def weight_high(name):
                for kt in range(KT):
                    n = FIRST[name] + kt
                    act.wait_ge(turned, n + 1)
                    act.activation(wT_of(W_INDEX[name], HI)[:, kt], ps[:, kt % T_BANKS], ACT.Copy,
                                   scale=WEIGHT_SCALE).then_inc(turned_hi, 1)

            def relative_table():
                for k in range(REL_ITEMS):
                    act.wait_ge(turned, FIRST["rel"] + k + 1)
                    act.activation(rel_rev[:, k * 512:(k + 1) * 512], ps[0:s.H, k % T_BANKS],
                                   ACT.Copy, scale=SCORE_SCALE).then_inc(turned_hi, 1)

            def turned_high(first, dst):
                for kt in range(KT):
                    act.wait_ge(turned, first + kt + 1)
                    act.copy(dst[:, HI, kt], ps[:, kt % T_BANKS]).then_inc(turned_hi, 1)

            def project_high(c, which, tiles=range(TT)):
                for j in tiles:
                    item = which * TT + j
                    act.wait_ge(multiplied, c * M_CHUNK + item + 1)
                    bank = ps[:, 4 + item % M_BANKS]
                    if which == 1:
                        if later(c):
                            act.wait_ge(v_stored, c * TT * DMA)
                        act.activation(v_out[:, j], bank, ACT.Copy, scale=1 / WEIGHT_SCALE).then_inc(product_hi, 1)
                    else:
                        if which == 2:
                            act.wait_ge(k_stored, (c + 1) * TT * DMA)
                        elif later(c):
                            act.wait_ge(q_stored, c * TT * DMA)
                        scale = 1 / WEIGHT_SCALE if which == 0 else SCORE_SCALE * s.DK**-0.5 / WEIGHT_SCALE
                        act.activation(qk_cut[:, j, HI], bank, ACT.Copy, scale=scale).then_inc(product_hi, 1)

            weight_high("wk")
            turned_high(ctx_item(0), cT)
            project_high(0, 0, [0, 1])
            weight_high("wv")
            project_high(0, 0, [2, 3])
            project_high(0, 1, [0])
            turned_high(x_item(0), xT)
            project_high(0, 1, [1])
            weight_high("wq")
            project_high(0, 1, [2])
            weight_high("wo")
            project_high(0, 1, [3])
            relative_table()

            def rest(c, more):
                if more:
                    turned_high(ctx_item(c + 1), cT)
                project_high(c, 2)
                if more:
                    turned_high(x_item(c + 1), xT)

            def chunk(c, more):
                project_high(c, 0)
                project_high(c, 1)
                if not more:
                    act.wait_ge(b1_turned, 1)
                    act.copy(keep["b1T"][:], ps[:, 1, 0:P]).then_inc(b1_kept, 1)
                rest(c, more)

            rest(0, True)
            with act.Fori(1, NCH - 1) as c:
                chunk(c, True)
            chunk(NCH - 1, False)

        @block.vector
        def _(dve):
            dve.memset(rel_raw[:], 0.0).then_inc(rel_zeroed, 1)
            dve.memset(m_min[:], 1.0).then_inc(mask_min_done, 1)

            def weight_low(name):
                w = W_INDEX[name]
                for kt in range(KT):
                    dve.wait_ge(turned_hi, FIRST[name] + kt + 1)
                    dve.scalar_tensor_tensor(out=wT_of(w, LO)[:, kt], in0=ps[:, kt % T_BANKS], scalar=WEIGHT_SCALE,
                                             in1=wT_of(w, HI)[:, kt], op0=ALU.mult, op1=ALU.subtract).then_inc(turned_lo, 1)

            def statistics(c):
                dve.wait_ge(x_loaded, (c + 1) * DMA)
                for t in range(TT):
                    dve.bn_stats(stats[:, t], x_in[:, t]).then_inc(stats_done, 1)
                dve.wait_ge(stats_done, (c + 1) * TT)
                settle(dve, dve_gate)
                for t in range(TT):
                    ins = dve.bn_aggr(moments[:, t], stats[:, t])
                ins.then_inc(moments_done, 1)

            def smallest_mask(c):
                dve.wait_ge(m_loaded, (c + 1) * DMA)
                dve.wait_ge(mask_min_done, c + 1)
                dve.tensor_reduce(m_new[:], m_in[:], AXIS.XY, ALU.min).then_inc(mask_read, 1)
                dve.wait_ge(mask_read, c + 1)
                dve.tensor_tensor(m_min[:], m_min[:], m_new[:], ALU.min).then_inc(mask_min_done, 1)

            def normalize(c):
                dve.wait_ge(rstd_done, c + 1)
                if later(c):
                    dve.wait_ge(turned, FIRST["x"] + KT if isinstance(c, int) and c == 1 else SETUP + c * T_CHUNK)
                for t in range(TT):
                    dve.tensor_scalar(x_norm[:, t], x_in[:, t], moments[:, t, 0:1], rstd[:, t:t + 1],
                                      ALU.subtract, ALU.mult).then_inc(x_normed, 1)

            def turned_low(first, dst):
                for kt in range(KT):
                    dve.wait_ge(turned_hi, first + kt + 1)
                    dve.tensor_tensor(dst[:, LO, kt], ps[:, kt % T_BANKS], dst[:, HI, kt],
                                      ALU.subtract).then_inc(turned_lo, 1)

            def project_low(c, which, tiles=range(TT)):
                for j in tiles:
                    item = which * TT + j
                    dve.wait_ge(product_hi, c * M_CHUNK + item + 1)
                    scale = 1 / WEIGHT_SCALE if which == 0 else SCORE_SCALE * s.DK**-0.5 / WEIGHT_SCALE
                    dve.scalar_tensor_tensor(out=qk_cut[:, j, LO], in0=ps[:, 4 + item % M_BANKS], scalar=scale,
                                             in1=qk_cut[:, j, HI], op0=ALU.mult, op1=ALU.subtract).then_inc(product_lo, 1)

            weight_low("wk")
            turned_low(ctx_item(0), cT)
            project_low(0, 0, [0, 1])
            weight_low("wv")
            statistics(0)
            project_low(0, 0, [2, 3])
            normalize(0)
            turned_low(x_item(0), xT)
            weight_low("wq")
            weight_low("wo")

            def rest(c, more):
                if more:
                    if later(c):
                        smallest_mask(c + 1)
                    normalize(c + 1)
                    turned_low(ctx_item(c + 1), cT)
                if not later(c):
                    smallest_mask(0)
                project_low(c, 2)
                if more:
                    turned_low(x_item(c + 1), xT)
                if not later(c):
                    smallest_mask(1)

            def chunk(c, more):
                if more:
                    statistics(c + 1)
                project_low(c, 0)
                if not more:
                    dve.wait_ge(flag_turned, 1)
                    dve.tensor_reduce(keep["all_kept"][:], ps[0:1, 0, 0:P], AXIS.X, ALU.min).then_inc(flag_kept, 1)
                    dve.wait_ge(flag_kept, 1)
                rest(c, more)

            statistics(1)
            rest(0, True)
            with dve.Fori(1, NCH - 1) as c:
                chunk(c, True)
            chunk(NCH - 1, False)

        @block.tensor
        def _(pe):
            ident, exchange = keep["ident"], keep["exchange"]
            pe.wait_ge(consts_ready, 10)

            def banks_free(n, low):
                pe.wait_ge(turned_hi, n - T_BANKS + 1)
                pe.wait_ge(turned_lo, low - T_BANKS + 1)

            def turn_weight(name):
                pe.wait_ge(w_loaded[W_INDEX[name]], DMA)
                for kt in range(KT):
                    if FIRST[name] > 0:
                        banks_free(FIRST[name] + kt, FIRST[name] + kt)
                    for j in range(4):
                        ins = pe.transpose(ps[:, kt % T_BANKS, j * P:(j + 1) * P],
                                           w_raw[:, W_INDEX[name], j, kt * P:(kt + 1) * P], ident[:])
                    ins.then_inc(turned, 1)

            def turn_relative_table():
                pe.wait_ge(rel_loaded, 2 * DMA)
                for k in range(REL_ITEMS):
                    banks_free(FIRST["rel"] + k, FIRST["rel"] + k)
                    for j in range(4):
                        z = k * 4 + j
                        ins = pe.transpose(ps[0:s.H, k % T_BANKS, j * P:(j + 1) * P],
                                           rel_raw[:, s.REL // P - 1 - z, :], exchange[:])
                    ins.then_inc(turned, 1)

            def turn(first, low, src, perm):
                for kt in range(KT):
                    banks_free(first + kt, low + kt)
                    for t in range(TT):
                        ins = pe.transpose(ps[:, kt % T_BANKS, t * P:(t + 1) * P], src[:, t, kt * P:(kt + 1) * P], perm[:])
                    ins.then_inc(turned, 1)

            def turn_ctx(c):
                pe.wait_ge(c_loaded, (c + 1) * DMA)
                turn(ctx_item(c), low_item(c, ctx_item(c)), c_in, ident)

            def turn_x(c):
                pe.wait_ge(x_normed, (c + 1) * TT)
                turn(x_item(c), low_item(c, x_item(c)), x_norm, exchange)

            def bank_free(c, which, j):
                item = which * TT + j
                if which == 0:
                    if later(c):
                        pe.wait_ge(product_hi, c * M_CHUNK)
                        pe.wait_ge(product_lo, c * 2 * TT)
                    return
                pe.wait_ge(product_hi, c * M_CHUNK + item - M_BANKS + 1)
                if which == 1:
                    pe.wait_ge(product_lo, c * 2 * TT + j + 1)

            def project_T(c, which, w, src, tiles=range(TT)):
                for j in tiles:
                    bank_free(c, which, j)
                    bank = ps[:, 4 + (which * TT + j) % M_BANKS]
                    steps = [(kt, a, b) for kt in range(KT) for a, b in PASSES]
                    for n, (kt, a, b) in enumerate(steps):
                        ins = pe.matmul(bank, wT[:, w, a, kt, j * P:(j + 1) * P], src[:, b, kt],
                                        start=(n == 0), stop=(n == len(steps) - 1))
                    ins.then_inc(multiplied, 1)

            def project_v(c, tiles=range(TT)):
                for j in tiles:
                    bank_free(c, 1, j)
                    bank = ps[:, 4 + (TT + j) % M_BANKS]
                    steps = [(kt, a, b) for kt in range(KT) for a, b in PASSES]
                    for n, (kt, a, b) in enumerate(steps):
                        ins = pe.matmul(bank, cT[:, a, kt, j * P:(j + 1) * P], wT[:, 2, b, kt],
                                        start=(n == 0), stop=(n == len(steps) - 1))
                    ins.then_inc(multiplied, 1)

            def cut_complete(c, item):
                pe.wait_ge(turned_hi, item + KT)
                pe.wait_ge(turned_lo, low_item(c, item) + KT)

            def rest(c, more):
                if more:
                    turn_ctx(c + 1)
                cut_complete(c, x_item(c) if later(c) else FIRST["wq"])
                project_T(c, 2, 0, xT)
                if more:
                    turn_x(c + 1)

            def chunk(c, more):
                cut_complete(c, ctx_item(c))
                project_T(c, 0, 1, cT)
                project_v(c)
                if not more:
                    pe.wait_ge(turned_hi, SETUP + NCH * T_CHUNK)
                    pe.wait_ge(turned_lo, W_ITEMS + NCH * T_CHUNK)
                    pe.wait_ge(b1_loaded, DMA)
                    pe.transpose(ps[:, 1, 0:P], b1_raw[:], ident[:]).then_inc(b1_turned, 1)
                    pe.wait_ge(mask_min_done, NCH + 1)
                    pe.transpose(ps[0:1, 0, 0:P], m_min[:], ident[:]).then_inc(flag_turned, 1)
                rest(c, more)

            turn_weight("wk")
            turn_ctx(0)
            cut_complete(0, ctx_item(0))
            project_T(0, 0, 1, cT, [0, 1])
            turn_weight("wv")
            project_T(0, 0, 1, cT, [2, 3])
            cut_complete(0, FIRST["wv"])
            project_v(0, [0])
            turn_x(0)
            project_v(0, [1])
            turn_weight("wq")
            project_v(0, [2])
            turn_weight("wo")
            project_v(0, [3])
            turn_relative_table()
            rest(0, True)
            with pe.Fori(1, NCH - 1) as c:
                chunk(c, True)
            chunk(NCH - 1, False)

        HEAD = s.DK * s.S
        half = s.S // CH

        def store_cut(sp, c, j, scratch_tensor):
            return sp.dma_start(
                bass.AP(scratch_tensor, (c // half) * (s.H * HEAD) + (c % half) * CH + j * s.HG * HEAD,
                        [[s.S, P], [s.NH * HEAD, 2], [1, CH]]), qk_cut[:, j])

        @block.sync
        def _(sp):
            def load_weight(name):
                w = W_INDEX[name]
                sp.dma_start(w_raw[:, w], weight_src[w].rearrange("(o p) i -> p o i", p=P)).then_inc(w_loaded[w], DMA)

            load_weight("wk")
            sp.dma_start(c_in[:], ctx_rows[0]).then_inc(c_loaded, DMA)
            load_weight("wv")
            load_weight("wq")
            load_weight("wo")
            sp.wait_ge(rel_zeroed, 1)
            full = (s.REL // P - 1) * P
            sp.dma_start(rel_raw[:, 0:s.REL // P - 1, :],
                         io["rel_emb"][0:full, :].rearrange("(t p) h -> p t h", p=P)).then_inc(rel_loaded, DMA)
            sp.dma_start(rel_raw[0:P - 1, s.REL // P - 1, :], io["rel_emb"][full:, :]).then_inc(rel_loaded, DMA)
            sp.dma_start(b1_raw[:], io["b1"].rearrange("e (f p) -> (e f) p", p=P)).then_inc(b1_loaded, DMA)

            def chunk(c, more):
                if more:
                    sp.wait_ge(turned, ctx_item(c) + KT)
                    sp.dma_start(c_in[:], ctx_rows[c + 1]).then_inc(c_loaded, DMA)
                for j in range(TT):
                    sp.wait_ge(product_lo, c * 2 * TT + j + 1)
                    store_cut(sp, c, j, scratch["k"]).then_inc(k_stored, DMA)
                for j in range(TT):
                    sp.wait_ge(product_hi, c * M_CHUNK + TT + j + 1)
                    sp.dma_start(
                        bass.AP(scratch["v"], (c // half) * (s.H * s.S * s.DK) + ((c % half) * CH + j * P) * s.DK,
                                [[s.DK, P], [s.S * s.DK, s.H], [1, s.DK]]), v_out[:, j]).then_inc(v_stored, DMA)
                for j in range(TT):
                    sp.wait_ge(product_lo, c * 2 * TT + TT + j + 1)
                    store_cut(sp, c, j, scratch["q"]).then_inc(q_stored, DMA)

            chunk(0, True)
            sp.wait_ge(turned_hi, FIRST["rel"] + REL_ITEMS)
            for b in range(s.B):
                sp.dma_start(scratch["rel"][b * s.H:(b + 1) * s.H, :], rel_rev[:]).then_inc(rel_rev_stored, DMA)
            with sp.Fori(1, NCH - 1) as c:
                chunk(c, True)
            sp.wait_ge(rel_rev_stored, s.B * DMA)
            for stored in (q_stored, k_stored, v_stored):
                sp.wait_ge(stored, (NCH - 1) * TT * DMA)
            for p in range(2):
                load_scores_operands(sp, s, scratch, keep, p, p)
                load_skew(sp, s, scratch, keep, p, p)
                load_values(sp, s, scratch, keep, p, p)
            chunk(NCH - 1, False)
            for stored in (k_stored, v_stored):
                sp.wait_ge(stored, NCH * TT * DMA)



def load_scores_operands(sp, s, scratch, keep, n, p):
    HEAD = s.DK * s.S
    for r in range(2):
        rows = slice(2 * s.DK * r, 2 * s.DK * (r + 1))
        sp.dma_start(keep["q_parts"][rows, p], bass.AP(scratch["q"], n * HEAD, [[s.NH * HEAD, 2], [s.S, s.DK], [1, s.S]])
                     ).then_inc(keep["q_loaded"][p], DMA)
        sp.dma_start(keep["k_parts"][rows, p], bass.AP(scratch["k"], r * s.NH * HEAD + n * HEAD,
                                                       [[0, 2], [s.S, s.DK], [1, s.S]])
                     ).then_inc(keep["k_loaded"][p], DMA)


def load_skew(sp, s, scratch, keep, n, p):
    sp.dma_start(keep["skew"][:, p], bass.AP(scratch["rel"].tensor, n * s.REL + 1, [[1, P], [1, s.SKEW]])
                 ).then_inc(keep["skew_loaded"][p], DMA)


def load_values(sp, s, scratch, keep, n, p):
    sp.dma_start(keep["v_head"][:, p], bass.AP(scratch["v"], n * s.S * s.DK, [[s.DK, P], [P * s.DK, s.QT], [1, s.DK]])
                 ).then_inc(keep["v_loaded"][p], DMA)


def cut_and_store_head(pool, s, scratch, keep, m, p):
    o_head, o_cut, o_high, o_low = keep["o_head"], keep["o_cut"], keep["o_high"], keep["o_low"]
    QC = s.S // 4
    pool.wait_ge(keep["o_ready"], m + 2)
    settle(pool, keep["pool_gate"])
    pool.tensor_copy(o_cut[:, p, HI], o_head[:, p]).then_inc(o_high, 1)
    pool.wait_ge(o_high, m + 1)
    pool.tensor_tensor(o_cut[:, p, LO], o_head[:, p], o_cut[:, p, HI], ALU.subtract).then_inc(o_low, 1)
    pool.wait_ge(o_low, m + 2)
    for part in (HI, LO):
        pool.dma_start(bass.AP(scratch["o"], part * s.T * s.D + m * s.DK * s.S, [[QC, 4], [s.S, s.DK], [1, QC]]),
                       o_cut[:, p, part]).then_inc(keep["o_stored"][p], DMA)



def load_weight_pair(sp, s, io, keep, e, k):
    slot = k % s.STAGES
    w_in, loaded = keep["weights_in"].rearrange("p w (m n) -> p w m n", m=2), keep["pair_loaded"][slot]
    sp.dma_start(w_in[:, slot, 0].rearrange("p (k f) -> p k f", k=s.KT),
                 bass.AP(io["w1"].tensor, e * s.D * s.F + k * 2 * P, [[s.F, P], [P * s.F, s.KT], [1, 2 * P]])
                 ).then_inc(loaded, DMA)
    sp.dma_start(w_in[:, slot, 1].rearrange("p (f d) -> p f d", f=2),
                 bass.AP(io["w2"].tensor, e * s.D * s.F + k * 2 * P * s.D, [[s.D, P], [P * s.D, 2], [1, s.D]])
                 ).then_inc(loaded, DMA)


def load_residual(eng, s, io, keep, e, loaded):
    x_rows = io["x"].rearrange("b s d -> (b s) d").rearrange("(c t p) d -> c p t d", t=s.TT, p=P)
    eng.dma_start(keep["x_res"][:], x_rows[e]).then_inc(loaded, DMA)


def load_attention(eng, s, scratch, keep, e, loaded):
    half = s.S // s.CH
    for part in (HI, LO):
        eng.dma_start(keep["o_in"][:, part], bass.AP(
            scratch["o"], part * s.T * s.D + (e // half) * (s.D * s.S) + (e % half) * s.CH,
            [[s.S, P], [P * s.S, s.KT], [1, s.CH]])).then_inc(loaded, DMA)


def attend_phase(nc, s, io, scratch, keep):
    NH, S, QT, DK = s.NH, s.S, s.QT, s.DK
    LAG = 3
    HEAD = DK * S
    CHUNKS = 4
    QC = S // CHUNKS

    items, first_item = [], []
    for t in range(QT):
        first_item.append(len(items))
        items += [("half", t, 0), ("half", t, 1)]
        if t == 3:
            items.append(("sums", t, 0))
        if t == 5:
            items.append(("spread", t, 0))
    PER = len(items)
    T_BANKS = 3
    assert PER % T_BANKS == 0
    ACT_HALVES = {(t, 0) for t in range(QT)} | {(3, 1)}

    spread_idx = items.index(("spread", 5, 0))
    sums_idx = items.index(("sums", 3, 0))

    def item_exists_at(n, idx):
        return not isinstance(n, int) or item_exists(n, idx)

    def by_act(idx):
        kind, t, h = items[idx]
        return kind != "half" or (t, h) in ACT_HALVES

    def item_exists(n, idx):
        kind, t, _ = items[idx]
        behind = 1 if kind != "half" or t < LAG else 0
        return 0 <= n - behind < NH

    def count(n, idx, engine=None):
        def upto(m, k):
            return sum(1 for a in range(m + 1) for j in range(PER if a < m else k + 1)
                       if item_exists(a, j) and (engine is None or by_act(j) == (engine == "act")))
        if isinstance(n, int):
            while idx < 0:
                n, idx = n - 1, idx + PER
            return upto(n, idx)
        back = 0
        while idx < 0:
            back, idx = back + 1, idx + PER
        per = upto(4, idx) - upto(3, idx)
        return n * per + (upto(4 - back, idx) - 4 * per)

    def before_in_bank(n, idx):
        back = 0
        k = idx - T_BANKS
        while True:
            m, j = back, k
            while j < 0:
                m, j = m + 1, j + PER
            if not isinstance(n, int):
                return k
            if n - m < 0:
                return None
            if item_exists(n - m, j):
                return k
            k -= T_BANKS

    VALUES_NEXT = {t: t - LAG for t in range(LAG, QT)}
    VALUES_AFTER = {t: QT - LAG + t for t in range(LAG)}

    with ExitStack() as ctx:
        sb = lambda name, shape, dt: ctx.enter_context(nc.sbuf_tensor(name, shape, dt))
        sem = lambda name: ctx.enter_context(nc.semaphore(name))
        q_parts, k_parts, v_head, skew = keep["q_parts"], keep["k_parts"], keep["v_head"], keep["skew"]
        biased = sb("biased", [P, 4, S], F32)
        neg_max = sb("neg_max", [P, 2 * QT], F32)
        probs = sb("probs", [P, 4, S], F32)
        row_sum = sb("row_sum", [P, 2, QT], F32)
        recip = sb("recip", [P, 2, QT], F32)
        recip_scaled_up = sb("recip_scaled_up", [P, QT], F32)
        recip_cut = sb("recip_cut", [P, 2, 2, QT], F16)
        recip_T = sb("recip_T", [2 * QT, P], F16)
        spread = sb("spread", [P, 2, QC], F32)
        probs_T = sb("probs_T", [P, 2, QT, S], F32)
        o_head = keep["o_head"]
        mask_u = sb("mask_u", [P, 2, S], U8)
        penalty = sb("penalty", [P, 2, S], BF16)
        ps = ctx.enter_context(nc.psum_tensor("ps_attend", [P, 8, 512], F32))
        values = ps[:, 7, 0:QC]

        pair = lambda name: [sem(f"{name}0"), sem(f"{name}1")]
        q_loaded, k_loaded, v_loaded, skew_loaded = (
            keep["q_loaded"], keep["k_loaded"], keep["v_loaded"], keep["skew_loaded"])
        scores_ready = sem("scores_ready")
        bias_done = sem("bias_done")
        probs_ready = sem("probs_ready")
        item_ready = sem("item_ready")
        read_act, read_dve = sem("read_act"), sem("read_dve")
        recip_done = sem("recip_done")
        recip_scaled, recip_high, recip_low = sem("recip_scaled"), sem("recip_high"), sem("recip_low")
        values_ready = sem("values_ready")
        o_ready = keep["o_ready"]
        o_low = keep["o_low"]
        o_stored = keep["o_stored"]
        mask_in = pair("mask_in")
        penalty_ready = sem("penalty_ready")
        pool_gate, dve_gate = keep["pool_gate"], sem("dve_gate2")

        def loops(eng, head, tail):
            for p in range(2):
                head(0, p)
            with eng.Fori(1, NH // 2) as i:
                for p in range(2):
                    head(i, p)
            if tail:
                for p in range(2):
                    head(NH // 2, p)

        def real(n, behind=0):
            return not isinstance(n, int) or 0 <= n - behind < NH

        def wait_read(pe, n, idx):
            prev = before_in_bank(n, idx)
            if prev is None:
                return
            engine = "act" if by_act(prev % PER) else "dve"
            pe.wait_ge(read_act if engine == "act" else read_dve, count(n, prev, engine))

        block = ctx.enter_context(nc.Block())

        @block.sync
        def _(sp):
            def head(i, p):
                n = i * 2 + p
                sp.wait_ge(scores_ready, QT * n - QT)
                load_scores_operands(sp, s, scratch, keep, n, p)
                sp.wait_ge(bias_done, QT * n - QT)
                load_skew(sp, s, scratch, keep, n, p)
                sp.wait_ge(values_ready, n - 1)
                load_values(sp, s, scratch, keep, n, p)

            sp.wait_ge(keep["q_stored"], s.NCH * s.TT * DMA)
            load_residual(sp, s, io, keep, 0, keep["x_first_loaded"])
            for k in range(s.STAGES):
                load_weight_pair(sp, s, io, keep, 0, k)
            with sp.Fori(1, NH // 2) as i:
                for p in range(2):
                    head(i, p)
            for p in range(2):
                sp.wait_ge(o_stored[p], s.H * DMA)
            load_attention(sp, s, scratch, keep, 0, keep["o_first_loaded"])

        @block.gpsimd
        def _(pool):
            all_kept = pool.value_load(keep["all_kept"][0:1, 0:1])
            pool.sem_inc(o_low, 1)

            def cut_reciprocals(n, p):
                pool.wait_ge(recip_done, n)
                settle(pool, pool_gate)
                pool.tensor_scalar(recip_scaled_up[:], recip[:, 1 - p], RECIP_SCALE, 0.0, ALU.mult, ALU.add
                                   ).then_inc(recip_scaled, 1)
                pool.wait_ge(recip_scaled, n)
                settle(pool, pool_gate)
                pool.tensor_copy(recip_cut[:, 1 - p, HI], recip_scaled_up[:]).then_inc(recip_high, 1)
                pool.wait_ge(recip_high, n)
                pool.tensor_tensor(recip_cut[:, 1 - p, LO], recip_scaled_up[:], recip_cut[:, 1 - p, HI],
                                   ALU.subtract).then_inc(recip_low, 1)

            def penalties(i, p, t):
                n = i * 2 + p
                slot = t % 2
                if real(n, 1) or t >= 2:
                    pool.wait_ge(scores_ready, QT * n + t - 1)
                rows = (n // s.H) * (S * S) + t * P * S
                pool.dma_start(mask_u[:, slot], bass.AP(io["mask"].tensor, rows, [[S, P], [1, S]])
                               ).then_inc(mask_in[slot], DMA)
                pool.wait_ge(mask_in[slot], (n * (QT // 2) + t // 2 + 1) * DMA)
                settle(pool, pool_gate)
                pool.tensor_scalar(penalty[:, slot], mask_u[:, slot], -MASKED, MASKED, ALU.mult, ALU.add
                                   ).then_inc(penalty_ready, 1)

            def head(i, p, masked):
                n = i * 2 + p
                for t in range(QT):
                    if masked and real(n):
                        penalties(i, p, t)
                    if t == 2 and real(n, 1):
                        cut_reciprocals(n, p)
                    if t == 5 and real(n, 2) and real(n):
                        cut_and_store_head(pool, s, scratch, keep, n - 2, p)
                    if t == QT - 1 and real(n, 2) and real(n):
                        pool.wait_ge(o_stored[p], i * 2 * DMA)

            with pool.If(all_kept == 1):
                loops(pool, lambda i, p: head(i, p, False), True)
            with pool.Else():
                loops(pool, lambda i, p: head(i, p, True), True)

        @block.vector
        def _(dve):
            dve.sem_inc(o_ready, 1)

            def head(i, p):
                n = i * 2 + p
                for t in range(QT):
                    if t == LAG and real(n, 2):
                        dve.wait_ge(values_ready, n - 1)
                        dve.wait_ge(read_act, count(n, spread_idx - PER, "act"))
                        if real(n):
                            dve.wait_ge(o_low, n - 1)
                        else:
                            dve.wait_ge(o_low, n - 2)
                        dve.scalar_tensor_tensor(out=o_head[:, p], in0=values, scalar=OUT_SCALE / RECIP_SCALE, in1=spread[:, p],
                                                 op0=ALU.mult, op1=ALU.mult).then_inc(o_ready, 1)
                    if real(n):
                        if t == 0:
                            dve.wait_ge(skew_loaded[p], (i + 1) * DMA)
                        dve.wait_ge(scores_ready, QT * n + t + 1)
                        if real(n, 1) or t >= 4:
                            dve.wait_ge(probs_ready, QT * n + t - 3)
                        settle(dve, dve_gate)
                        col = p * QT + t
                        at = S - P - t * P
                        dve.tensor_tensor_reduce(
                            out=biased[:, t % 4], in0=ps[:, 2 * (t % 2):2 * (t % 2) + 2].rearrange("p b k -> p (b k)"),
                            in1=skew[:, p, at:at + S], scale=-1 / SCORE_SCALE, scalar=3e38, op0=ALU.add, op1=ALU.min,
                            accum_out=neg_max[:, col:col + 1]).then_inc(bias_done, 1)
                    if t == 1 and real(n, 1):
                        dve.wait_ge(probs_ready, QT * n)
                        dve.reciprocal(recip[:, 1 - p], row_sum[:, 1 - p]).then_inc(recip_done, 1)
                    for idx in range(first_item[t], PER if t == QT - 1 else first_item[t + 1]):
                        kind, _, h = items[idx]
                        if by_act(idx) or not item_exists_at(n, idx):
                            continue
                        m_par = p if t >= LAG else 1 - p
                        unit = (t - LAG) % QT
                        dve.wait_ge(item_ready, count(n, idx))
                        if unit == 0 and real(n, 2):
                            dve.wait_ge(values_ready, n - 1)
                        dve.tensor_copy(probs_T[:, m_par, 4 * h:4 * h + 4, unit * P:(unit + 1) * P],
                                        ps[:, 4 + idx % T_BANKS].rearrange("p (k q) -> p k q", q=P)
                                        ).then_inc(read_dve, 1)
            loops(dve, head, True)

        @block.scalar
        def _(act):
            def head(i, p):
                n = i * 2 + p
                for t in range(QT):
                    if real(n, 1 if t == 0 else 0):
                        unit, par = (t - 1) % QT, p if t > 0 else 1 - p
                        col = par * QT + unit
                        act.wait_ge(bias_done, QT * n + t)
                        if real(n, 1) or t >= 5:
                            last = first_item[(t - 2) % QT] + 1 - (PER if t < 2 else 0)
                            act.wait_ge(item_ready, count(n, last))
                        if t == 1 and real(n, 2):
                            act.wait_ge(recip_done, n - 1)
                        act.activation(probs[:, unit % 4], biased[:, unit % 4], ACT.Exp, bias=neg_max[:, col:col + 1],
                                       scale=-1.0, accum_out=row_sum[:, par, unit:unit + 1]).then_inc(probs_ready, 1)
                    for idx in range(first_item[t], PER if t == QT - 1 else first_item[t + 1]):
                        kind, _, h = items[idx]
                        if not by_act(idx) or not item_exists_at(n, idx):
                            continue
                        bank = ps[:, 4 + idx % T_BANKS]
                        act.wait_ge(item_ready, count(n, idx))
                        if kind == "half":
                            m_par = p if t >= LAG else 1 - p
                            unit = (t - LAG) % QT
                            if unit == 0 and real(n, 2):
                                act.wait_ge(values_ready, n - 1)
                            act.copy(probs_T[:, m_par, 4 * h:4 * h + 4, unit * P:(unit + 1) * P],
                                     bank.rearrange("p (k q) -> p k q", q=P)).then_inc(read_act, 1)
                        elif kind == "sums":
                            act.copy(recip_T[:], bank[0:2 * QT, 0:P]).then_inc(read_act, 1)
                        else:
                            if real(n, 2):
                                act.wait_ge(o_ready, n - 1)
                            act.copy(spread[:, 1 - p], bank[:, 0:QC]).then_inc(read_act, 1)
            loops(act, head, True)

        @block.tensor
        def _(pe):
            exchange, exchange_b, exchange_h = keep["exchange"], keep["exchange_b"], keep["exchange_h"]
            select = keep["select"]
            all_kept = pe.value_load(keep["all_kept"][0:1, 0:1])

            def weighted_values(i_of, par, n, kt):
                if kt == 0:
                    pe.wait_ge(v_loaded[par], (i_of + 1) * DMA)
                    for name, sem_ in (("act", read_act), ("dve", read_dve)):
                        pe.wait_ge(sem_, count(n, first_item[LAG] - 1, name))
                    if real(n, 2):
                        pe.wait_ge(o_ready, n)
                for c in range(CHUNKS):
                    ins = pe.matmul(values[c * DK:(c + 1) * DK], v_head[:, par, kt],
                                    probs_T[:, par, kt, c * QC:(c + 1) * QC],
                                    start=(kt == 0), stop=(kt == QT - 1))
                if kt == QT - 1:
                    ins.then_inc(values_ready, 1)

            def head(i, p, masked):
                n = i * 2 + p
                for t in range(QT):
                    slot = t % 2
                    if real(n):
                        if t == 0:
                            pe.wait_ge(q_loaded[p], (i + 1) * 2 * DMA)
                            pe.wait_ge(k_loaded[p], (i + 1) * 2 * DMA)
                        if real(n, 1) or t >= 2:
                            pe.wait_ge(bias_done, QT * n + t - 1)
                        if masked:
                            pe.wait_ge(penalty_ready, QT * n + t + 1)
                        for k in range(S // 512):
                            bank = ps[:, 2 * slot + k]
                            ins = pe.matmul(bank, q_parts[:, p, t * P:(t + 1) * P],
                                            k_parts[:, p, k * 512:(k + 1) * 512], start=True, stop=not masked)
                            if masked:
                                ins = pe.matmul(bank, exchange_b[:], penalty[:, slot, k * 512:(k + 1) * 512],
                                                start=False, stop=True)
                        ins.then_inc(scores_ready, 1)
                    for idx in range(first_item[t], PER if t == QT - 1 else first_item[t + 1]):
                        kind, _, h = items[idx]
                        if not item_exists_at(n, idx):
                            continue
                        bank = ps[:, 4 + idx % T_BANKS]
                        wait_read(pe, n, idx)
                        if kind == "half":
                            if h == 0:
                                pe.wait_ge(probs_ready, QT * n + t - LAG + 1)
                            for k in range(4):
                                kt = 4 * h + k
                                ins = pe.transpose(bank[:, k * P:(k + 1) * P],
                                                   probs[:, (t - LAG) % 4, kt * P:(kt + 1) * P], exchange[:])
                        elif kind == "sums":
                            pe.wait_ge(recip_low, n)
                            ins = pe.matmul(bank[0:2 * QT, 0:P], recip_cut[:, 1 - p].rearrange("p a u -> p (a u)"),
                                            exchange_h[:], start=True, stop=True)
                        else:
                            pe.wait_ge(read_act, count(n, sums_idx, "act"))
                            for u in range(2):
                                ins = pe.matmul(bank[:, u * P:(u + 1) * P],
                                                select[:, u].rearrange("r c d -> r (c d)"), recip_T[:],
                                                start=True, stop=True)
                        ins.then_inc(item_ready, 1)
                    if t in VALUES_NEXT and real(n, 1):
                        weighted_values(i if p == 1 else i - 1, 1 - p, n, VALUES_NEXT[t])
                    if t in VALUES_AFTER and real(n, 2):
                        weighted_values(i - 1, p, n, VALUES_AFTER[t])

            with pe.If(all_kept == 1):
                loops(pe, lambda i, p: head(i, p, False), True)
            with pe.Else():
                loops(pe, lambda i, p: head(i, p, True), True)


def feed_phase(nc, s, io, scratch, keep):
    KT, TT, CH, D, FT, E = s.KT, s.TT, s.CH, s.D, s.FT, s.E
    PAIRS = FT // 2
    STAGES = s.STAGES
    with ExitStack() as ctx:
        sb = lambda name, shape, dt: ctx.enter_context(nc.sbuf_tensor(name, shape, dt))
        sem = lambda name: ctx.enter_context(nc.semaphore(name))
        w_raw = keep["weights_in"].rearrange("p w (m n) -> p w m n", m=2)
        w1c = sb("w1_cut", [P, PAIRS, 2, KT, 2 * P], F16)
        w2c = sb("w2_cut", [P, PAIRS, 2, 2, D], F16)
        o_in, x_in = keep["o_in"], keep["x_res"]
        b2_row = sb("b2_row", [P, D], F32)
        x_new = sb("x_new", [P, TT, D], F32)
        x_cur = sb("x_cur", [P, TT, D], F32)
        stats = sb("stats2", [P, TT, 6], F32)
        moments = sb("moments2", [P, TT, 2], F32)
        var_eps = sb("var_eps2", [P, TT], F32)
        rstd = sb("rstd2", [P, TT], F32)
        minus_half = sb("minus_half2", [P, TT], F32)
        x_norm = sb("x_norm2", [P, TT, D], F32)
        xT = sb("xT2", [P, 2, KT, CH], F16)
        hidden = sb("hidden", [P, 4, CH], F32)
        h_cut = sb("h_cut", [P, 4, 2, CH], F16)
        y_out = sb("y_out", [P, TT, D], F32)
        ps = ctx.enter_context(nc.psum_tensor("ps_feed", [P, 8, 512], F32))

        pair_loaded = keep["pair_loaded"]
        w_high, w_low = sem("w_high"), sem("w_low")
        o_loaded, x_loaded, b2_loaded = sem("o_loaded"), sem("x_res_loaded"), sem("b2_loaded")
        half_ready = sem("half_ready")
        pool_gate, dve_gate = keep["pool_gate"], sem("dve_gate3")
        projected = sem("projected")
        x_new_done, x_cur_done = sem("x_new_done"), sem("x_cur_done")
        stats_done, moments_done, normed = sem("stats2_done"), sem("moments2_done"), sem("x2_normed")
        var_done, rstd_done = sem("var2_done"), sem("rstd2_done")
        turned, turned_hi, turned_lo = sem("turned2"), sem("turned2_hi"), sem("turned2_lo")
        hidden_ready = sem("hidden_ready")
        gelu_done = sem("gelu_done")
        h_high, h_low = sem("h_high"), sem("h_low")
        slice_used = sem("slice_used")
        y_done = sem("y_done")
        y_stored, last_y_stored = sem("y_stored"), sem("last_y_stored")
        last_tile_used = sem("last_tile_used")

        out_rows = io["out"].rearrange("b s d -> (b s) d").rearrange("(c t p) d -> c p t d", t=TT, p=P)
        STEPS = FT + 2

        def turn_bank(e, kt):
            return 6 + kt % 2 if later(e) else kt

        PROJECT_AT = {3: 0, 5: 1, 7: 2, 9: 3}
        NORM_AT = 12
        TURN_AT = {FT - 1: [0, 1], FT: [2, 3]}
        OWN_CUTS = {False: {0: [2], 1: [3], 2: [4, 5], 3: [6, 7]}, True: {1: [PAIRS - 1]}}
        CUT_AT = {2 * k + 4: k for k in range(PAIRS - 1)}

        block = ctx.enter_context(nc.Block())

        @block.sync
        def _(sp):
            def load_pair(e, k):
                done = (e * PAIRS + k - STAGES + 1) * 2
                sp.wait_ge(w_high, done)
                sp.wait_ge(w_low, done)
                load_weight_pair(sp, s, io, keep, e, k)
            for k in range(STAGES, PAIRS):
                load_pair(0, k)
            with sp.Fori(1, E) as e:
                for k in range(PAIRS):
                    load_pair(e, k)
            for t in range(TT):
                sp.wait_ge(y_done, (E - 1) * TT + t + 1)
                sp.dma_start(out_rows[E - 1][:, t], y_out[:, t]).then_inc(last_y_stored, DMA)
            sp.wait_ge(last_y_stored, TT * DMA)

        @block.gpsimd
        def _(pool):
            pool.memset(minus_half[:], -0.5).then_inc(half_ready, 1)
            pool.wait_ge(half_ready, 1)
            for p in range(2):
                pool.wait_ge(keep["o_stored"][p], (s.NH - 2) * DMA)
                cut_and_store_head(pool, s, scratch, keep, s.NH - 2 + p, p)
            def rstd_of(e):
                pool.wait_ge(moments_done, e + 1)
                settle(pool, pool_gate)
                pool.tensor_scalar(var_eps[:], moments[:, :, 1], 1.0, EPS, ALU.mult, ALU.add).then_inc(var_done, 1)
                pool.wait_ge(var_done, e + 1)
                pool.tensor_tensor(rstd[:], var_eps[:], minus_half[:], ALU.pow).then_inc(rstd_done, 1)

            def load_b2(e):
                if later(e):
                    pool.wait_ge(x_cur_done, e * TT)
                pool.dma_start(b2_row[:], bass.AP(io["b2"].tensor, e * D, [[0, P], [1, D]])).then_inc(b2_loaded, DMA)

            def load_next(e):
                pool.wait_ge(projected, e * TT)
                pool.wait_ge(x_new_done, e * TT)
                load_residual(pool, s, io, keep, e, x_loaded)
                load_attention(pool, s, scratch, keep, e, o_loaded)

            def store(e):
                pool.wait_ge(y_done, (e + 1) * TT)
                pool.dma_start(out_rows[e], y_out[:]).then_inc(y_stored, DMA)

            load_b2(0)
            rstd_of(0)
            for stored in keep["o_stored"]:
                pool.wait_ge(stored, s.NH * DMA)
            load_next(1)
            load_b2(1)
            rstd_of(1)
            with pool.Fori(1, E - 1) as e:
                load_next(e + 1)
                store(e - 1)
                load_b2(e + 1)
                rstd_of(e + 1)
            store(E - 2)
            pool.wait_ge(y_stored, (E - 1) * DMA)

        @block.scalar
        def _(act):
            def cut_high(e, k):
                slot = k % STAGES
                act.wait_ge(pair_loaded[slot], (e * (PAIRS // STAGES) + k // STAGES + 1) * 2 * DMA)
                if later(e):
                    act.wait_ge(slice_used, (e - 1) * FT + 2 * k + 2)
                act.activation(w1c[:, k, HI], w_raw[:, slot, 0].rearrange("p (k f) -> p k f", k=KT), ACT.Copy,
                               scale=WEIGHT_SCALE).then_inc(w_high, 1)
                act.activation(w2c[:, k, HI], w_raw[:, slot, 1].rearrange("p (f d) -> p f d", f=2), ACT.Copy,
                               scale=WEIGHT_SCALE).then_inc(w_high, 1)

            def turned_high(e, kt):
                act.wait_ge(turned, e * KT + kt + 1)
                act.copy(xT[:, HI, kt], ps[:, turn_bank(e, kt)]).then_inc(turned_hi, 1)

            def frame(e, more):
                for f in range(STEPS):
                    if f < FT:
                        act.wait_ge(hidden_ready, e * FT + f + 1)
                        if f >= 4:
                            act.wait_ge(h_low, e * FT + f - 3)
                        elif later(e):
                            act.wait_ge(h_low, e * FT)
                        bias = keep["b1T"][:, bass.ds(e * FT + f, 1)]
                        act.activation(hidden[:, f % 4], ps[:, 4 + f % 2], ACT.Gelu_apprx_tanh, bias=bias,
                                       scale=1 / WEIGHT_SCALE).then_inc(gelu_done, 1)
                    for k in OWN_CUTS[later(e)].get(f, []):
                        cut_high(e, k)
                    if more and f in CUT_AT:
                        cut_high(e + 1, CUT_AT[f])
                    if more and f in TURN_AT:
                        for kt in TURN_AT[f]:
                            turned_high(e + 1, kt)

            cut_high(0, 0)
            for kt in range(KT):
                turned_high(0, kt)
            cut_high(0, 1)
            frame(0, True)
            with act.Fori(1, E - 1) as e:
                frame(e, True)
            frame(E - 1, False)

        @block.vector
        def _(dve):
            def cut_low(e, k):
                slot = k % STAGES
                done = (e * PAIRS + k) * 2
                dve.wait_ge(w_high, done + 1)
                dve.scalar_tensor_tensor(out=w1c[:, k, LO], in0=w_raw[:, slot, 0].rearrange("p (k f) -> p k f", k=KT),
                                         scalar=WEIGHT_SCALE, in1=w1c[:, k, HI], op0=ALU.mult, op1=ALU.subtract
                                         ).then_inc(w_low, 1)
                dve.wait_ge(w_high, done + 2)
                dve.scalar_tensor_tensor(out=w2c[:, k, LO], in0=w_raw[:, slot, 1].rearrange("p (f d) -> p f d", f=2),
                                         scalar=WEIGHT_SCALE, in1=w2c[:, k, HI], op0=ALU.mult, op1=ALU.subtract
                                         ).then_inc(w_low, 1)

            def residual(e, t):
                if t == 0:
                    if later(e):
                        dve.wait_ge(x_loaded, e * DMA)
                    else:
                        dve.wait_ge(keep["x_first_loaded"], DMA)
                dve.wait_ge(projected, e * TT + t + 1)
                dve.scalar_tensor_tensor(out=x_new[:, t], in0=ps[:, 6 + t % 2], scalar=1 / (WEIGHT_SCALE * OUT_SCALE),
                                         in1=x_in[:, t], op0=ALU.mult, op1=ALU.add).then_inc(x_new_done, 1)
                dve.wait_ge(x_new_done, e * TT + t + 1)
                dve.bn_stats(stats[:, t], x_new[:, t]).then_inc(stats_done, 1)

            def aggregate(e):
                dve.wait_ge(stats_done, (e + 1) * TT)
                settle(dve, dve_gate)
                for t in range(TT):
                    ins = dve.bn_aggr(moments[:, t], stats[:, t])
                ins.then_inc(moments_done, 1)

            def normalize(e):
                dve.wait_ge(rstd_done, e + 1)
                for t in range(TT):
                    dve.tensor_scalar(x_norm[:, t], x_new[:, t], moments[:, t, 0:1], rstd[:, t:t + 1],
                                      ALU.subtract, ALU.mult).then_inc(normed, 1)

            def turned_low(e, kt):
                dve.wait_ge(turned_hi, e * KT + kt + 1)
                dve.tensor_tensor(xT[:, LO, kt], ps[:, turn_bank(e, kt)], xT[:, HI, kt], ALU.subtract).then_inc(turned_lo, 1)

            def add_b2(e):
                dve.wait_ge(b2_loaded, (e + 1) * DMA)
                if later(e):
                    dve.wait_ge(y_done, e * TT)
                for t in range(TT):
                    dve.tensor_tensor(x_cur[:, t], x_new[:, t], b2_row[:], ALU.add).then_inc(x_cur_done, 1)

            def output(e):
                last = isinstance(e, int) and e == E - 1
                if not last:
                    dve.wait_ge(slice_used, (e + 1) * FT)
                if later(e):
                    dve.wait_ge(y_stored, e * DMA)
                dve.wait_ge(x_cur_done, (e + 1) * TT)
                for t in range(TT):
                    if last:
                        dve.wait_ge(last_tile_used, t + 1)
                    dve.scalar_tensor_tensor(out=y_out[:, t], in0=ps[:, t], scalar=1 / WEIGHT_SCALE, in1=x_cur[:, t],
                                             op0=ALU.mult, op1=ALU.add).then_inc(y_done, 1)

            def frame(e, more):
                for f in range(STEPS):
                    for k in OWN_CUTS[later(e)].get(f, []):
                        cut_low(e, k)
                    if f < FT:
                        dve.wait_ge(gelu_done, e * FT + f + 1)
                        if f >= 4:
                            dve.wait_ge(slice_used, e * FT + f - 3)
                        elif later(e):
                            dve.wait_ge(slice_used, e * FT)
                        dve.tensor_copy(h_cut[:, f % 4, HI], hidden[:, f % 4]).then_inc(h_high, 1)
                        dve.wait_ge(h_high, e * FT + f + 1)
                        dve.tensor_tensor(h_cut[:, f % 4, LO], hidden[:, f % 4], h_cut[:, f % 4, HI],
                                          ALU.subtract).then_inc(h_low, 1)
                    if more and f in CUT_AT:
                        cut_low(e + 1, CUT_AT[f])
                    if more and f in PROJECT_AT:
                        residual(e + 1, PROJECT_AT[f])
                    if more and f == 9:
                        aggregate(e + 1)
                    if more and f == NORM_AT:
                        normalize(e + 1)
                    if more and f in TURN_AT:
                        for kt in TURN_AT[f]:
                            turned_low(e + 1, kt)
                    if f == 1 and not later(e):
                        add_b2(e)
                output(e)
                if more:
                    add_b2(e + 1)

            residual(0, 0)
            cut_low(0, 0)
            for t in range(1, TT):
                residual(0, t)
            aggregate(0)
            normalize(0)
            for kt in range(KT):
                turned_low(0, kt)
            cut_low(0, 1)
            frame(0, True)
            with dve.Fori(1, E - 1) as e:
                frame(e, True)
            frame(E - 1, False)

        @block.tensor
        def _(pe):
            woT, ident = keep["woT"], keep["ident"]
            last_pass = len(PASSES) - 1

            def project(e, t):
                if t == 0:
                    if later(e):
                        pe.wait_ge(o_loaded, e * 2 * DMA)
                    else:
                        pe.wait_ge(keep["o_first_loaded"], 2 * DMA)
                if t < 2:
                    if later(e):
                        pe.wait_ge(turned_lo, e * KT)
                else:
                    pe.wait_ge(x_new_done, e * TT + t - 1)
                steps = [(kt, a, b) for kt in range(KT) for a, b in PASSES]
                for n, (kt, a, b) in enumerate(steps):
                    ins = pe.matmul(ps[:, 6 + t % 2], o_in[:, a, kt, t * P:(t + 1) * P], woT[:, b, kt],
                                    start=(n == 0), stop=(n == len(steps) - 1))
                ins.then_inc(projected, 1)

            def turn(e, kt):
                if kt == 0:
                    pe.wait_ge(normed, (e + 1) * TT)
                if kt < 2 and later(e):
                    pe.wait_ge(x_new_done, e * TT + 3 + kt)
                elif later(e):
                    pe.wait_ge(turned_lo, e * KT + kt - 1)
                for t in range(TT):
                    ins = pe.transpose(ps[:, turn_bank(e, kt), t * P:(t + 1) * P], x_norm[:, t, kt * P:(kt + 1) * P], ident[:])
                ins.then_inc(turned, 1)

            def first(e, f):
                if f == 0:
                    pe.wait_ge(turned_lo, (e + 1) * KT)
                if f % 2 == 0:
                    pe.wait_ge(w_low, (e * PAIRS + f // 2 + 1) * 2)
                if later(e) or f >= 2:
                    pe.wait_ge(gelu_done, e * FT + (f - 1 if f >= 2 else 0))
                steps = [(kt, a, b) for kt in range(KT) for a, b in PASSES]
                for n, (kt, a, b) in enumerate(steps):
                    ins = pe.matmul(ps[:, 4 + f % 2], w1c[:, f // 2, a, kt, (f % 2) * P:(f % 2 + 1) * P], xT[:, b, kt],
                                    start=(n == 0), stop=(n == len(steps) - 1))
                ins.then_inc(hidden_ready, 1)

            def second(e, f):
                pe.wait_ge(h_low, e * FT + f + 1)
                if f == 0 and later(e):
                    pe.wait_ge(y_done, e * TT)
                for t in range(TT):
                    for n, (a, b) in enumerate(PASSES):
                        ins = pe.matmul(ps[:, t], h_cut[:, f % 4, a, t * P:(t + 1) * P], w2c[:, f // 2, b, f % 2],
                                        start=(f == 0 and n == 0), stop=(f == FT - 1 and n == last_pass))
                    if isinstance(e, int) and e == E - 1 and f == FT - 1:
                        ins.then_inc(last_tile_used, 1)
                if not (isinstance(e, int) and e == E - 1 and f == FT - 1):
                    ins.then_inc(slice_used, 1)

            def frame(e, more):
                for f in range(STEPS):
                    if f < FT:
                        first(e, f)
                    if more and f in PROJECT_AT:
                        project(e + 1, PROJECT_AT[f])
                    if more and f in TURN_AT:
                        for kt in TURN_AT[f]:
                            turn(e + 1, kt)
                    if f >= 2:
                        second(e, f - 2)

            for t in range(TT):
                project(0, t)
            for kt in range(KT):
                turn(0, kt)
            frame(0, True)
            with pe.Fori(1, E - 1) as e:
                frame(e, True)
            frame(E - 1, False)


def build(nc, io):
    s = Shapes(io["x"], io["rel_emb"], io["w1"])
    scratch = {
        "q": nc.dram_tensor("q_scratch", [2, s.NH * s.DK, s.S], F16),
        "k": nc.dram_tensor("k_scratch", [2, s.NH * s.DK, s.S], F16),
        "v": nc.dram_tensor("v_scratch", [s.NH, s.S, s.DK], F32),
        "o": nc.dram_tensor("o_scratch", [2, s.NH * s.DK, s.S], F16),
        "rel": nc.dram_tensor("rel_scratch", [s.NH, s.REL], F32).ap(),
    }
    with ExitStack() as ctx:
        sb = lambda name, shape, dt: ctx.enter_context(nc.sbuf_tensor(name, shape, dt))
        sem = lambda name: ctx.enter_context(nc.semaphore(name))
        keep = {
            "ident": sb("ident", [P, P], F32),
            "exchange": sb("exchange", [P, P], F32),
            "exchange_b": sb("exchange_b", [P, P], BF16),
            "exchange_h": sb("exchange_h", [P, P], F16),
            "select": sb("select", [2 * s.QT, 2, 4, s.DK], F16),
            "woT": sb("woT", [P, 2, s.KT, s.D], F16),
            "b1T": sb("b1T", [P, s.E * s.FT], F32),
            "all_kept": sb("all_kept", [1, 1], I32),
            "weights_in": sb("weights_in", [P, 4, 4 * s.D], F32),
            "pair_loaded": [sem(f"pair_loaded{k}") for k in range(s.STAGES)],
            "x_res": sb("x_res", [P, s.TT, s.D], F32), "x_first_loaded": sem("x_first_loaded"),
            "o_in": sb("o_in", [P, 2, s.KT, s.CH], F16), "o_first_loaded": sem("o_first_loaded"),
            "o_head": sb("o_head", [P, 2, s.S // 4], F32), "o_ready": sem("o_ready"),
            "o_cut": sb("o_cut", [P, 2, 2, s.S // 4], F16), "o_high": sem("o_high"), "o_low": sem("o_low"),
            "pool_gate": sem("pool_gate"), "o_stored": [sem("o_out0"), sem("o_out1")],
        }
        with ExitStack() as ctx2:
            sb = lambda name, shape, dt: ctx2.enter_context(nc.sbuf_tensor(name, shape, dt))
            pair = lambda name: [ctx2.enter_context(nc.semaphore(f"{name}{p}")) for p in range(2)]
            keep |= {
                "q_parts": sb("q_parts", [P, 2, s.S], F16), "q_loaded": pair("q_in"),
                "k_parts": sb("k_parts", [P, 2, s.S], F16), "k_loaded": pair("k_in"),
                "v_head": sb("v_head", [P, 2, s.QT, s.DK], F32), "v_loaded": pair("v_in"),
                "skew": sb("skew", [P, 2, s.SKEW], F32), "skew_loaded": pair("skew_in"),
                "qk_cut": sb("qk_cut", [P, s.TT, 2, s.CH], F16),
                "q_stored": ctx2.enter_context(nc.semaphore("q_stored")),
            }
            project_phase(nc, s, io, scratch, keep)
            attend_phase(nc, s, io, scratch, keep)
        feed_phase(nc, s, io, scratch, keep)


_NAMES = {
    "x": "x", "ctx": "ctx_1024", "mask": "mask_Bx1xSxS2_bf1", "wq": "L0_xattn_w_q", "wk": "L0_xattn_w_k",
    "wv": "L0_xattn_w_v", "wo": "L0_xattn_w_o", "rel_emb": "L0_xattn_rel_emb", "w1": "L0_ffn_w1",
    "b1": "L0_ffn_b1", "w2": "L0_ffn_w2", "b2": "L0_ffn_b2",
}


def kernel(**inputs):
    import numpy as np
    import concourse.bacc as bacc
    from concourse.bass_utils import run_bass_kernel_spmd

    nc = bacc.Bacc("TRN2", target_bir_lowering=False, num_devices=1)
    arrays, io = {}, {}
    for short, name in _NAMES.items():
        a = np.ascontiguousarray(inputs[name])
        if a.dtype == bool:
            a = a.view(np.uint8)
        arrays[f"in_{short}"] = a
        io[short] = nc.dram_tensor(f"in_{short}", a.shape, mybir.dt.from_np(a.dtype), kind="ExternalInput").ap()
    io["out"] = nc.dram_tensor("out_0", inputs["x"].shape, F32, kind="ExternalOutput").ap()
    build(nc, io)
    r = run_bass_kernel_spmd(nc, [arrays], core_ids=[0])
    return r.results[0]["out_0"]
```
